# Optimizing a Trainium2 kernel written in Bass

```python
import numpy as np
import jax
import jax.numpy as jnp

def _softmax(x, axis=-1):
    return jax.nn.softmax(x, axis=axis)

def _gelu(x):
    return jax.nn.gelu(x, approximate=True)

def _silu(x):
    return jax.nn.silu(x)

def _sigmoid(x):
    return jax.nn.sigmoid(x)

def _layernorm(x, axis=-1, eps=1e-05):
    m = jnp.mean(x, axis=axis, keepdims=True)
    v = jnp.var(x, axis=axis, keepdims=True)
    return (x - m) / jnp.sqrt(v + eps)

def _scatter_add(tgt, idx, src, axis=0):
    return tgt.at[idx].add(src)

def _segment_sum(src, seg, n):
    return jax.ops.segment_sum(src, seg, n)
kernel_name = 'mk_macaron_d1_jaxref_r4_090946'

def setup_inputs(seed: int=0):
    np.random.seed(seed)
    _w = jnp.asarray

    def _L0_attn_setup():
        import jax, jax.numpy as jnp
        import numpy as np
        NUM_HEADS = 16
        D_MODEL = 256
        HEAD_DIM = D_MODEL // NUM_HEADS
        NEG_INF = -1000000000.0

        def alibi_bidirectional_bias(num_heads, seq_len, dtype=jnp.float32):
            half = num_heads // 2
            base = 24.0 ** (1.0 / half)
            slopes = (1.0 / base ** jnp.arange(1, half + 1, dtype=dtype))[:, None, None]
            pos = jnp.arange(seq_len)
            rel = (pos[None, :] - pos[:, None]).astype(dtype)
            neg = jnp.full((seq_len, seq_len), NEG_INF, dtype=dtype)
            fwd = slopes * jnp.tril(rel) + jnp.triu(neg, 1)
            bwd = slopes * jnp.triu(-rel) + jnp.tril(neg, -1)
            return jnp.concatenate([fwd, bwd], axis=0)
        key = jax.random.key(seed)
        ks = jax.random.split(key, 9)
        B, S, D = (2, 512, D_MODEL)
        sc = 1.0 / np.sqrt(D)
        inp = {'x': jax.random.normal(ks[0], (B, S, D), dtype=jnp.float32)}
        inp['Wq'] = jax.random.normal(ks[1], (D, D), dtype=jnp.float32) * sc
        inp['bq'] = jnp.zeros((D,), dtype=jnp.float32)
        inp['Wk'] = jax.random.normal(ks[2], (D, D), dtype=jnp.float32) * sc
        inp['bk'] = jnp.zeros((D,), dtype=jnp.float32)
        inp['Wv'] = jax.random.normal(ks[3], (D, D), dtype=jnp.float32) * sc
        inp['bv'] = jnp.zeros((D,), dtype=jnp.float32)
        inp['Wf'] = jax.random.normal(ks[4], (D, D), dtype=jnp.float32) * sc
        inp['bf'] = jnp.zeros((D,), dtype=jnp.float32)
        return inp
    _L0_attn_in = _L0_attn_setup()

    def _L0_ffn_setup():
        import jax, jax.numpy as jnp
        import numpy as np
        HIDDEN = 256
        N_ROUTED = 16
        N_SHARED = 2
        TOP_K = 2
        MID_R = HIDDEN // 4
        MID_S = HIDDEN // 2
        key = jax.random.key(seed)
        ks = jax.random.split(key, 8)
        s = 0.02
        return {'x': jax.random.normal(ks[0], (2, 256, HIDDEN), dtype=jnp.float32), 'router_w': jax.random.normal(ks[1], (HIDDEN, N_ROUTED), dtype=jnp.float32) * s, 'wg_r': jax.random.normal(ks[2], (N_ROUTED, HIDDEN, MID_R), dtype=jnp.float32) * s, 'wu_r': jax.random.normal(ks[3], (N_ROUTED, HIDDEN, MID_R), dtype=jnp.float32) * s, 'wd_r': jax.random.normal(ks[4], (N_ROUTED, MID_R, HIDDEN), dtype=jnp.float32) * s, 'wg_s': jax.random.normal(ks[5], (N_SHARED, HIDDEN, MID_S), dtype=jnp.float32) * s, 'wu_s': jax.random.normal(ks[6], (N_SHARED, HIDDEN, MID_S), dtype=jnp.float32) * s, 'wd_s': jax.random.normal(ks[7], (N_SHARED, MID_S, HIDDEN), dtype=jnp.float32) * s}
    _L0_ffn_in = _L0_ffn_setup()
    _d = {'L0_attn_x': _L0_attn_in['x'], 'L0_attn_Wq': _L0_attn_in['Wq'], 'L0_attn_bq': _L0_attn_in['bq'], 'L0_attn_Wk': _L0_attn_in['Wk'], 'L0_attn_bk': _L0_attn_in['bk'], 'L0_attn_Wv': _L0_attn_in['Wv'], 'L0_attn_bv': _L0_attn_in['bv'], 'L0_attn_Wf': _L0_attn_in['Wf'], 'L0_attn_bf': _L0_attn_in['bf'], 'L0_ffn_router_w': _L0_ffn_in['router_w'], 'L0_ffn_wg_r': _L0_ffn_in['wg_r'], 'L0_ffn_wu_r': _L0_ffn_in['wu_r'], 'L0_ffn_wd_r': _L0_ffn_in['wd_r'], 'L0_ffn_wg_s': _L0_ffn_in['wg_s'], 'L0_ffn_wu_s': _L0_ffn_in['wu_s'], 'L0_ffn_wd_s': _L0_ffn_in['wd_s']}
    _x0 = _d['L0_attn_x']
    _d['L0_attn_x'] = jax.random.normal(jax.random.fold_in(jax.random.key(seed), 1), (16, 512, 256), dtype=_x0.dtype)
    del _x0
    return _d

def reference(L0_attn_x, L0_attn_Wq, L0_attn_bq, L0_attn_Wk, L0_attn_bk, L0_attn_Wv, L0_attn_bv, L0_attn_Wf, L0_attn_bf, L0_ffn_router_w, L0_ffn_wg_r, L0_ffn_wu_r, L0_ffn_wd_r, L0_ffn_wg_s, L0_ffn_wu_s, L0_ffn_wd_s):

    def _L0_attn_ref(x, Wq, bq, Wk, bk, Wv, bv, Wf, bf):
        import jax, jax.numpy as jnp
        import numpy as np
        NUM_HEADS = 16
        D_MODEL = 256
        HEAD_DIM = D_MODEL // NUM_HEADS
        NEG_INF = -1000000000.0

        def alibi_bidirectional_bias(num_heads, seq_len, dtype=jnp.float32):
            half = num_heads // 2
            base = 24.0 ** (1.0 / half)
            slopes = (1.0 / base ** jnp.arange(1, half + 1, dtype=dtype))[:, None, None]
            pos = jnp.arange(seq_len)
            rel = (pos[None, :] - pos[:, None]).astype(dtype)
            neg = jnp.full((seq_len, seq_len), NEG_INF, dtype=dtype)
            fwd = slopes * jnp.tril(rel) + jnp.triu(neg, 1)
            bwd = slopes * jnp.triu(-rel) + jnp.tril(neg, -1)
            return jnp.concatenate([fwd, bwd], axis=0)
        B, S, D = x.shape
        H, hd = (NUM_HEADS, HEAD_DIM)

        def heads(y):
            return y.reshape(B, S, H, hd).transpose(0, 2, 1, 3)
        q = heads(x @ Wq + bq)
        k = heads(x @ Wk + bk)
        v = heads(x @ Wv + bv)
        bias = alibi_bidirectional_bias(H, S, x.dtype)
        scores = jnp.einsum('bhqd,bhkd->bhqk', q, k) * (1.0 / np.sqrt(hd)) + bias[None]
        attn = jax.nn.softmax(scores, axis=-1)
        out = jnp.einsum('bhqk,bhkd->bhqd', attn, v)
        out = out.transpose(0, 2, 1, 3).reshape(B, S, D)
        return out @ Wf + bf

    def _L0_ffn_ref(x, router_w, wg_r, wu_r, wd_r, wg_s, wu_s, wd_s):
        import jax, jax.numpy as jnp
        import numpy as np
        HIDDEN = 256
        N_ROUTED = 16
        N_SHARED = 2
        TOP_K = 2
        MID_R = HIDDEN // 4
        MID_S = HIDDEN // 2
        orig_shape = x.shape
        flat = x.reshape(-1, orig_shape[-1])
        gs = jnp.einsum('td,ndm->tnm', flat, wg_s)
        us = jnp.einsum('td,ndm->tnm', flat, wu_s)
        out = jnp.einsum('tnm,nmd->td', jax.nn.silu(gs) * us, wd_s)
        logits = (flat @ router_w).astype(jnp.float32)
        probs = jax.nn.softmax(logits, axis=-1)
        weights, indices = jax.lax.top_k(probs, TOP_K)
        weights = weights / (weights.sum(axis=-1, keepdims=True) + 1e-09)
        weights = weights.astype(x.dtype)
        comb = jnp.sum(jax.nn.one_hot(indices, N_ROUTED, dtype=x.dtype) * weights[..., None], axis=1)
        g = jnp.einsum('td,edm->tem', flat, wg_r)
        u = jnp.einsum('td,edm->tem', flat, wu_r)
        h = jax.nn.silu(g) * u
        h = h * comb[:, :, None]
        out = out + jnp.einsum('tem,emd->td', h, wd_r)
        return out.reshape(orig_shape)
    x = L0_attn_x
    x = x + 0.5 * _L0_ffn_ref(_layernorm(x, axis=-1), L0_ffn_router_w, L0_ffn_wg_r, L0_ffn_wu_r, L0_ffn_wd_r, L0_ffn_wg_s, L0_ffn_wu_s, L0_ffn_wd_s)
    x = x + _L0_attn_ref(_layernorm(x, axis=-1), L0_attn_Wq, L0_attn_bq, L0_attn_Wk, L0_attn_bk, L0_attn_Wv, L0_attn_bv, L0_attn_Wf, L0_attn_bf)
    x = x + 0.5 * _L0_ffn_ref(_layernorm(x, axis=-1), L0_ffn_router_w, L0_ffn_wg_r, L0_ffn_wu_r, L0_ffn_wd_r, L0_ffn_wg_s, L0_ffn_wu_s, L0_ffn_wd_s)
    return x

_drawn_inputs = setup_inputs


def setup_inputs(seed=0):
    import zlib

    import numpy as np

    out = dict(_drawn_inputs(seed))
    spreads = {'L0_attn_bq': (0.0, 0.31),
     'L0_attn_bk': (0.0, 0.8),
     'L0_attn_bv': (0.0, 0.1),
     'L0_attn_bf': (0.0, 0.1)}
    factors = {'L0_ffn_router_w': 8.0,
     'L0_ffn_wg_r': 8.0,
     'L0_ffn_wu_r': 8.0,
     'L0_ffn_wd_r': 8.0,
     'L0_ffn_wg_s': 3.715,
     'L0_ffn_wu_s': 3.663,
     'L0_ffn_wd_s': 3.669}
    for name, (base, spread) in spreads.items():
        noise = np.random.default_rng([zlib.crc32(name.encode()), seed]).standard_normal(out[name].shape)
        drawn = base * np.exp(spread * noise) if base else spread * noise
        out[name] = jnp.asarray(drawn.astype(out[name].dtype))
    for name, factor in factors.items():
        out[name] = (out[name] * factor).astype(out[name].dtype)
    return out
```

```python
from contextlib import ExitStack

import concourse.bass as bass
from concourse import mybir

F32 = mybir.dt.float32
F32R = mybir.dt.float32r
BF16 = mybir.dt.bfloat16
F16 = mybir.dt.float16
ALU = mybir.AluOpType
ACT = mybir.ActivationFunctionType
X = mybir.AxisListType.X

P = 128
B, S, D = 16, 512, 256
H, HD = 16, 16
NT = S // P
ND = D // P
E = 16
ME, MS = 64, 128
NM = 10
NSH = 2
ITERS = B // 2
NPAIR = H // 2
HB = P // HD
PARTS = 3
ROWS_S = 6 * HD + 3
ROWS_P = ROWS_S + 2
QB = (0, 0, 0, 1, 1, 2)
KB = (0, 1, 2, 0, 1, 0)
EPS = 1e-5
BIG = 1e30
N_CONST = 10
VW = 50

STAGES = (("ffn", 0), ("ffn", 1), ("att", 0), ("att", 1), ("ffn", 0), ("ffn", 1))
NS = len(STAGES)


class Book:

    def __init__(self):
        self.events = {}
        self.slots = {}
        self.final = False


class Signal:

    def __init__(self, ctx, nc, book, name, unit=1):
        self.sem = ctx.enter_context(nc.semaphore(name))
        self.name, self.unit, self.book = name, unit, book
        self.old = book.events.get(name, {})
        self.new = book.events[name] = {} if not book.final else self.old
        self.before, self.value = True, 0

    def step(self, *key):
        if self.before:
            if self.unit > 1:
                self.value += self.unit
                return self.sem, self.unit
            to = (self.old.get(key, 0) + 1) * self.unit
            by, self.value = max(to - self.value, self.unit), to
            return self.sem, by
        if not self.book.final:
            assert key not in self.new, (self.name, key)
            self.new[key] = len(self.new)
        return self.sem, self.unit

    def at(self, it, *key, prev=False):
        n, i = len(self.old), self.old.get(key)
        if self.book.final:
            assert i is not None, (self.name, key)
        else:
            return self.sem, 1
        if prev:
            it = it - 1
        return self.sem, (it + 1) * (n * self.unit) + (i + 1) * self.unit

    def enter_loop(self, eng):
        self.before = False
        rest = len(self.old) * self.unit - self.value
        if rest > 0:
            eng.sem_inc(self.sem, rest)


class Ring:

    def __init__(self, book, name, banks):
        self.book, self.name, self.banks = book, name, banks
        self.old = book.slots.get(name, [])
        if not book.final:
            book.slots[name] = []
        self.new = book.slots[name]
        self.early = {}
        self.order = {key: i for i, (key, _, _) in enumerate(self.old)}

    def bank(self, *key):
        return self.banks[self.order.get(key, 0) % len(self.banks)]

    def take(self, it, key, freed, freed_key, before=False):
        nb = len(self.banks)
        if before:
            i = self.order.get(key, 0) % nb
            wait = self.early.get(i)
            self.early[i] = (freed, freed_key)
            return wait[0].at(-1, *wait[1]) if wait else None
        if not self.book.final:
            self.new.append((key, freed.name, freed_key))
            return freed.sem, 1
        n = -(-len(self.old) // nb) * nb
        i = self.order[key] - nb
        while i % n >= len(self.old):
            i -= nb
        _, name, k = self.old[i % n]
        return self.signals[name].at(it, *k, prev=i < 0)


def build(nc, book, a, out):
    ctx = ExitStack()
    with ctx:
        def sb(name, shape, dt=F32):
            return ctx.enter_context(nc.sbuf_tensor(name, shape, dt))

        sigs = {}

        def signal(name, unit=1):
            sigs[name] = Signal(ctx, nc, book, name, unit)
            return sigs[name]

        def sem(name):
            return ctx.enter_context(nc.semaphore(name))

        bank = [ctx.enter_context(nc.psum_tensor(f"bank{i}", [P, 512], F32)) for i in range(8)]
        ring_u = Ring(book, "u", bank[0:3])
        ring_g = Ring(book, "g", bank[3:6])
        ring_y = Ring(book, "y", bank[6:8])

        w_gate = sb("w_gate", [P, 2, ND, NM * P], F32R)
        w_up = sb("w_up", [P, 2, ND, NM * P], F32R)
        w_down = sb("w_down", [P, 2, NM, D], F32R)
        w_attn = sb("w_attn", [P, 2, 4, ND, D], F32R)
        w_route = sb("w_route", [P, ND, P], F32R)
        x_tok = [sb(f"x_tok{s}", [P, NT, D]) for s in range(2)]
        x_in = [sb(f"x_in{s}", [P, NT, D]) for s in range(2)]
        xn_tok = sb("xn_tok", [P, NT, D])
        o_tok = sb("o_tok", [P, NT, D])
        act_t = [sb(f"act_t{i}", [P, 2, ND, S], F32R) for i in range(2)]
        q_stack = sb("q_stack", [P, H, S], BF16)
        k_stack = sb("k_stack", [P, H, S], BF16)
        v_parts = [sb(f"v_parts{i}", [P, NT, H, VW], BF16) for i in range(2)]
        work_at = -(-nc.sbuf_base // 32) * 32
        work = sb("work", [P, 6144])
        h_parts = nc.alloc_sbuf_tensor_at("h_parts", [P, 3, 2, S], F32R, offset=work_at + 2048 * 4)
        th_buf = [work[:, 512 * i:512 * (i + 1)] for i in range(2)]
        h_buf = [work[:, 1024 + 512 * i:1536 + 512 * i] for i in range(2)]
        hs_buf = [[h_parts[:, i, c, :] for c in range(2)] for i in range(3)]
        p_buf = [work[:, 512 * i:512 * (i + 1)] for i in range(2)]
        ps_buf = [[[work[:, 1024 + 2560 * i + 256 * (2 * t + c):1280 + 2560 * i + 256 * (2 * t + c)]
                    .bitcast(F16) for c in range(2)] for t in range(5)] for i in range(2)]
        stats = sb("stats", [P, NT, 6])
        mom = sb("mom", [P, 5, NT])
        mean = sb("mean", [P, NT])
        var_eps = sb("var_eps", [P, NT])
        rstd = sb("rstd", [P, NT])
        minus_half = sb("minus_half", [P, NT])
        logit = sb("logit", [P, NT, E])
        top = sb("top", [P, 8, NT])
        rt = sb("rt", [P, 6, NT, E])
        comb = sb("comb", [P, NT, P], F16)
        comb_t = [sb(f"comb_t{i}", [P, S], F16) for i in range(2)]
        qk_part = [sb(f"qk_part{i}", [P, PARTS, S], BF16) for i in range(2)]
        qk_rest = [sb(f"qk_rest{i}", [P, S]) for i in range(2)]
        v_tok = qk_rest[0][:, :].rearrange("p (t d) -> p t d", d=D)
        logit_t = qk_rest[1]
        row_max = [sb(f"row_max{i}", [P, 8]) for i in range(2)]
        shift = [sb(f"shift{i}", [P, 2, 8], BF16) for i in range(2)]
        shift_t = [sb(f"shift_t{i}", [16, P], BF16) for i in range(2)]
        o_sum = sb("o_sum", [P, 8, HD])
        o_rden = sb("o_rden", [P, 8])
        c32 = sb("c32", [P, P + NT * E])
        c16 = sb("c16", [P, P + 8 * P], F16)
        cbf = sb("cbf", [P, 3 * P], BF16)
        bias_qk = sb("bias_qk", [P, 2, ND])
        bias_v = sb("bias_v", [P, D])
        bias_f = sb("bias_f", [P, D])
        ident32, rev = c32[:, 0:P], c32[:, P:].rearrange("p (t e) -> p t e", e=E)
        ident16, select = c16[:, 0:P], c16[:, P:].rearrange("p (j m) -> p j m", m=P)
        ident_bf, mask_up, mask_low = cbf[:, 0:P], cbf[:, P:2 * P], cbf[:, 2 * P:]

        u_full, g_full, y_full = signal("u_full"), signal("g_full"), signal("y_full")
        h_used = signal("h_used")
        tanh_done, h_hi, act_hi = signal("tanh_done"), signal("h_hi"), signal("act_hi")
        logits_out, route_exp, comb_out = signal("logits_out"), signal("route_exp"), signal("comb_out")
        qk_first, qk_second = signal("qk_first"), signal("qk_second")
        v_first, v_second = signal("v_first"), signal("v_second")
        exp_done, exp_hi, shift_out = signal("exp_done"), signal("exp_hi"), signal("shift_out")
        h_step, act_lo, norm_step = signal("h_step"), signal("act_lo"), signal("norm_step")
        route_step, qk_step, v_step = signal("route_step"), signal("qk_step"), signal("v_step")
        max_done, shift_step, p_lo_v = signal("max_done"), signal("shift_step"), signal("p_lo_v")
        o_step, x_new = signal("o_step"), signal("x_new")
        rstd_done, h_lo, qk_third = signal("rstd_done"), signal("h_lo"), signal("qk_third")
        p_lo_g, bias_added = signal("p_lo_g"), signal("bias_added")
        x_loaded = [signal(f"x_loaded{s}", 16) for s in range(2)]
        stored = [signal(f"stored{s}", 16) for s in range(2)]
        scattered = {(w, m): signal(f"scattered_{w}{m}", 16) for m in range(2) for w in ("q", "k")}
        shift_row = [signal(f"shift_row{i}", 16) for i in range(2)]
        for r in (ring_u, ring_g, ring_y):
            r.signals = sigs
        stack_free = sem("stack_free")
        const_in, aug_in = sem("const_in"), sem("aug_in")
        raw_in = [sem(f"raw_in{i}") for i in range(7)]
        filled, w_hi_done, w_lo_done = sem("filled"), sem("w_hi_done"), sem("w_lo_done")
        ones_done = sem("ones_done")

        raw_gu = [t[:, :, :].rearrange("p h s -> p (h s)").bitcast(F32)[:, 0:ND * NM * P // 2]
                  for t in (q_stack, k_stack)]
        raw_att = work[:, 0:4 * ND * D].rearrange("p (w k n) -> p w k n", w=4, k=ND)
        raw_route = o_tok[:, 0, 0:ND * E].rearrange("p (k e) -> p k e", e=E)

        HALF = NM * P

        def piece(i):
            if i < 4:
                w = (w_gate, w_up)[i // 2]
                return w[:, 0, i % 2, :], w[:, 1, i % 2, :]
            half = slice(5 * (i - 4), 5 * (i - 4) + 5)
            return (w_down[:, 0, half, :].rearrange("p j n -> p (j n)"),
                    w_down[:, 1, half, :].rearrange("p j n -> p (j n)"))

        def raw(i):
            t = (q_stack, k_stack)[i // 3]
            flat = t[:, :, :].rearrange("p h s -> p (h s)").bitcast(F32)
            return flat[:, (i % 3) * HALF:(i % 3 + 1) * HALF]

        def att_dst(c, w, k):
            ap = w_attn[:, c, w, k, :]
            return ap.rearrange("p (m d h) -> p m h d", m=ND, h=HB) if w < 2 else \
                ap.rearrange("p (m h d) -> p m h d", m=ND, h=HB)

        def att_src(w, k):
            return raw_att[:, w, k, :].rearrange("p (m h d) -> p m h d", m=ND, h=HB)

        def forward(h):
            return h < H // 2

        def keys(h, qt):
            return (0, P * (qt + 1)) if forward(h) else (P * qt, S)

        def tile_of(pair, hh, r):
            kt = r if forward(2 * pair) else NT - 1 - r
            q0, q1 = (P * kt, S) if forward(2 * pair) else (0, P * (kt + 1))
            slot = {0: 3 * hh, 1: 3 * hh + 1, 2: 2, 3: 3 * hh + 1}[r]
            col = {0: 0, 1: 0, 2: 256 * hh, 3: 384}[r]
            return kt, slot, col, q0, q1

        def slot_tiles(pair, slot):
            return [(hh, r) for hh in range(2) for r in range(NT) if tile_of(pair, hh, r)[1] == slot]

        def last_stage(k):
            return (3, True) if k == 2 else (2, False)

        FFN_AT = {1: "norm", 4: "transpose", 5: "a", 6: "b", 9: "c"}
        ATT_AT = {2: "norm", 4: "transpose", 5: "a", 6: "b", 8: "c"}
        QK_ORDER = (("q", 0), ("k", 0), ("q", 1), ("k", 1))
        LO_ON_VECTOR = (2, 4)

        def prep_stage(k):
            return (k + 1) % NS

        def program(eng, signals, stage_ffn, stage_att, prep, flush, setup=None):
            for piece_name in ("norm", "transpose", "a", "b", "c"):
                prep[piece_name](-1, 0, True)
            if setup:
                setup()
            for s in signals:
                s.enter_loop(eng)
            with eng.Fori(0, ITERS) as it:
                for k, (kind, _) in enumerate(STAGES):
                    (stage_ffn if kind == "ffn" else stage_att)(it, k)
                flush(it, NS - 1)

        block = ctx.enter_context(nc.Block())

        @block.sync
        def _(sp):
            w = {n.replace("L0_ffn_", ""): ap for n, ap in a.items()}
            for dst, src in ((c32, a["c32"]), (c16, a["c16"]), (cbf, a["cbf"])):
                sp.dma_start(dst[:, :], src).then_inc(const_in, 16)
            sp.dma_start(raw_route, w["router_w"].rearrange("(k p) e -> p k e", p=P)).then_inc(const_in, 16)
            for i in range(6):
                if i < 4:
                    shared = w[("wg_s", "wu_s")[i // 2]][:, P * (i % 2):P * (i % 2) + P, :]
                    routed = w[("wg_r", "wu_r")[i // 2]][:, P * (i % 2):P * (i % 2) + P, :]
                    sp.dma_start(raw(i)[:, 0:NSH * P].rearrange("p (n m) -> p n m", n=NSH),
                                 shared.rearrange("n p m -> p n m")).then_inc(raw_in[i], 16)
                    sp.dma_start(raw(i)[:, NSH * P:].rearrange("p (e m) -> p e m", e=E),
                                 routed.rearrange("e p m -> p e m")).then_inc(raw_in[i], 16)
                else:
                    rows = w["wd_r"].rearrange("(j e) m d -> (e m) j d", e=2)
                    n_sh = NSH if i == 4 else 0
                    j0 = 0 if i == 4 else 5 - NSH
                    if n_sh:
                        sp.dma_start(raw(i)[:, 0:n_sh * D].rearrange("p (n d) -> p n d", n=n_sh),
                                     w["wd_s"].rearrange("n m d -> m n d")).then_inc(raw_in[i], 16)
                    sp.dma_start(raw(i)[:, n_sh * D:].rearrange("p (j d) -> p j d", d=D),
                                 rows[:, j0:j0 + 5 - n_sh, :]).then_inc(raw_in[i], 16)
            for i, n in enumerate(("Wq", "Wk", "Wv", "Wf")):
                sp.dma_start(raw_att[:, i, :, :],
                             a["L0_attn_" + n].rearrange("(k p) n -> p k n", p=P)).then_inc(raw_in[6], 16)
            for i, n in enumerate(("bq", "bk")):
                for m in range(ND):
                    sp.dma_start(bias_qk[:, i, m:m + 1],
                                 a["L0_attn_" + n][P * m:P * m + P].rearrange("(h d) -> d h", h=HB),
                                 allow_slow_non_contiguous=True).then_inc(const_in, 16)
            for dst, n in ((bias_v, "bv"), (bias_f, "bf")):
                sp.dma_start(dst[:, :], a["L0_attn_" + n].rearrange("(o d) -> o d", o=1)
                             .broadcast_to((P, D))).then_inc(const_in, 16)
            sp.wait_ge(w_hi_done, 15)
            sp.wait_ge(w_lo_done, 17)
            sp.dma_start(q_stack[6 * HD:ROWS_S, :, :], a["q_rows"]).then_inc(aug_in, 16)
            sp.dma_start(k_stack[6 * HD:ROWS_P, :, :], a["k_rows"]).then_inc(aug_in, 16)
            sp.wait_ge(aug_in, 32)

            for s in scattered.values():
                s.enter_loop(sp)

            def scatter(it, k):
                before, prev = last_stage(k)
                for n, (what, m) in enumerate(QK_ORDER):
                    sp.wait_ge(*g_full.at(it, "scores", before, 4 * m + 3, 4, prev=prev))
                    sp.sem_inc(stack_free, 1)
                    sp.wait_ge(*qk_third.at(it, k, what, m))
                    stack, parts = (q_stack, QB) if what == "q" else (k_stack, KB)
                    for blk in range(6):
                        sp.dma_start(stack[HD * blk:HD * blk + HD, HB * m:HB * m + HB, :],
                                     qk_part[n % 2][:, parts[blk], :]
                                     ).then_inc(*scattered[what, m].step(k, blk))

            with sp.Fori(0, ITERS) as it:
                scatter(it, 2)
                scatter(it, 3)

        @block.tensor
        def _(pe):
            def take(ring, it, key, freed, freed_key, before=False):
                wait = ring.take(it, key, freed, freed_key, before)
                if wait:
                    pe.wait_ge(*wait)
                return ring.bank(*key)

            def product(dst, left, right, first, last):
                pe.matmul(dst, left(0), right(0), start=first, stop=False, skip_group_check=True)
                pe.matmul(dst, left(0), right(1), start=False, stop=False, skip_group_check=True)
                return pe.matmul(dst, left(1), right(0), start=False, stop=last, skip_group_check=True)

            def transpose_act(it, key, src, par, freed_by, before=False):
                for d in range(ND):
                    ps = take(ring_u, it, (key, d), freed_by, (key, d), before)
                    for t in range(NT):
                        ins = pe.transpose(ps[:, P * t:P * t + P], src[:, t, P * d:P * d + P], ident32)
                    ins.then_inc(*u_full.step(key, d))

            def prep_norm(it, k, before=False):
                pass

            def prep_transpose(it, k, before=False):
                pe.wait_ge(*norm_step.at(it, k, "apply", NT - 1))
                if before:
                    pe.wait_ge(const_in, 16 * N_CONST)
                transpose_act(it, ("xn", k), xn_tok, k % 2, act_lo, before)

            def prep_a(it, k, before=False):
                pe.wait_ge(*act_lo.at(it, ("xn", k), ND - 1))
                pe.wait_ge(*act_hi.at(it, ("xn", k), ND - 1))
                xt = act_t[k % 2]
                if STAGES[k][0] == "ffn":
                    if before:
                        pe.wait_ge(w_lo_done, 3)
                    ps = take(ring_u, it, ("logits", k), logits_out, (k,), before)
                    for d in range(ND):
                        for c in range(2):
                            ins = pe.matmul(ps[:, :], w_route[:, d, :], xt[:, c, d, :],
                                            start=(d + c == 0), stop=(d + c == 2))
                    ins.then_inc(*u_full.step("logits", k))
                else:
                    qk_product(it, k, 0)

            def qk_product(it, k, m):
                xt = act_t[k % 2]
                for w, what in enumerate(("q", "k")):
                    ps = take(ring_g, it, (what, k, m), qk_step, (k, what, m))
                    for d in range(ND):
                        ins = product(ps[:, :], lambda c: w_attn[:, c, w, d, P * m:P * m + P],
                                      lambda c: xt[:, c, d, :], d == 0, d == ND - 1)
                    ins.then_inc(*g_full.step(what, k, m))

            def prep_b(it, k, before=False):
                if STAGES[k][0] == "ffn":
                    pe.wait_ge(*logits_out.at(it, k))
                    ps = take(ring_u, it, ("route", k), route_step, (k, "sum"), before)
                    for t in range(NT):
                        ins = pe.transpose(ps[:, P * t:P * t + P], logit_t[:, P * t:P * t + P], ident32)
                    ins.then_inc(*u_full.step("route", k))
                else:
                    xt = act_t[k % 2]
                    for half in range(2):
                        ps = take(ring_g, it, ("v", k, half), v_step, (k, half, "bias"))
                        for i in range(2):
                            t = 2 * half + i
                            for d in range(ND):
                                ins = product(ps[:, D * i:D * i + D],
                                              lambda c: xt[:, c, d, P * t:P * t + P],
                                              lambda c: w_attn[:, c, 2, d, :],
                                              i == 0 and d == 0, d == ND - 1)
                        ins.then_inc(*g_full.step("v", k, half))

            def prep_c(it, k, before=False):
                if STAGES[k][0] == "ffn":
                    pe.wait_ge(*route_step.at(it, k, "lo"))
                    ps = take(ring_u, it, ("comb", k), comb_out, (k,), before)
                    ps16 = ps[:, 0:S // 2].bitcast(F16)
                    for t in range(NT):
                        ins = pe.transpose(ps16[:, P * t:P * t + P], comb[:, t, :], ident16)
                    ins.then_inc(*u_full.step("comb", k))
                else:
                    qk_product(it, k, 1)

            prep = dict(norm=prep_norm, transpose=prep_transpose, a=prep_a, b=prep_b, c=prep_c)

            def down(it, k, j):
                pe.wait_ge(*h_lo.at(it, k, j))
                pe.wait_ge(*h_hi.at(it, k, j))
                hs = hs_buf[j % 3]
                for t in range(NT):
                    if j == 0 and t % 2 == 0:
                        take(ring_y, it, ("y", k, t // 2), x_new, (k, t // 2))
                    y = ring_y.bank("y", k, t // 2)[:, D * (t % 2):D * (t % 2) + D]
                    ins = product(y, lambda c: hs[c][:, P * t:P * t + P],
                                  lambda c: w_down[:, c, j, :], j == 0 and t % 2 == 0, j == NM - 1)
                    if j == NM - 1 and t % 2 == 1:
                        ins.then_inc(*y_full.step("y", k, t // 2))
                if j < NM - 1:
                    ins.then_inc(*h_used.step(k, j))

            def tail(it, k, part):
                if k < 0:
                    return
                if STAGES[k][0] == "ffn":
                    down(it, k, NM - 2 + part)
                elif part == 0:
                    pe.wait_ge(*o_step.at(it, k, NPAIR - 1, "out"))
                    transpose_act(it, ("o", k), o_tok, k % 2, act_lo)
                else:
                    pe.wait_ge(*act_lo.at(it, ("o", k), ND - 1))
                    pe.wait_ge(*act_hi.at(it, ("o", k), ND - 1))
                    ot = act_t[k % 2]
                    for half in range(2):
                        ps = take(ring_y, it, ("y", k, half), x_new, (k, half))
                        for i in range(2):
                            t = 2 * half + i
                            for d in range(ND):
                                ins = product(ps[:, D * i:D * i + D],
                                              lambda c: ot[:, c, d, P * t:P * t + P],
                                              lambda c: w_attn[:, c, 3, d, :],
                                              i == 0 and d == 0, d == ND - 1)
                        ins.then_inc(*y_full.step("y", k, half))

            def stage_ffn(it, k):
                xt = act_t[k % 2]
                pe.wait_ge(*act_lo.at(it, ("xn", k), ND - 1, prev=k == 0))
                pe.wait_ge(*act_hi.at(it, ("xn", k), ND - 1, prev=k == 0))
                for j in range(NM):
                    for ring, full, w, name, freed in ((ring_g, g_full, w_gate, "gate", "g"),
                                                       (ring_u, u_full, w_up, "up", "h" if j < NSH else "u")):
                        ps = take(ring, it, (name, k, j), h_step, (k, j, freed))
                        for d in range(ND):
                            ins = product(ps[:, :], lambda c: w[:, c, d, P * j:P * j + P],
                                          lambda c: xt[:, c, d, :], d == 0, d == ND - 1)
                        ins.then_inc(*full.step(name, k, j))
                    if j >= NSH:
                        if j == NSH:
                            pe.wait_ge(*comb_out.at(it, k, prev=k == 0))
                        ps = take(ring_u, it, ("weight", k, j), h_step, (k, j, "h"))
                        pe.matmul(ps[:, :], select[:, j - NSH, :], comb_t[k % 2][:, :],
                                  start=True, stop=True).then_inc(*u_full.step("weight", k, j))
                    if j < 2:
                        tail(it, k - 1, j)
                    else:
                        down(it, k, j - 2)
                    if j in FFN_AT:
                        prep[FFN_AT[j]](it, prep_stage(k))

            def score(it, k, p, i):
                hh, qt = i // NT, i % NT
                h = 2 * p + hh
                k0, k1 = keys(h, qt)
                ps = take(ring_u, it, ("max", k, p, i), max_done, (k, p, i))
                pe.matmul(ps[:, 0:k1 - k0], q_stack[0:ROWS_S, h, P * qt:P * qt + P],
                          k_stack[0:ROWS_S, h, k0:k1], start=True, stop=False, skip_group_check=True)
                c, mask = (P * qt - k0, mask_up) if forward(h) else (0, mask_low)
                pe.matmul(ps[:, c:c + P], ident_bf, mask, start=False, stop=True,
                          skip_group_check=True).then_inc(*u_full.step("max", k, p, i))

            def score_t(it, k, p, slot):
                ps = take(ring_g, it, ("scores", k, p, slot), exp_hi, (k, p, slot))
                for n, (hh, r) in enumerate(slot_tiles(p, slot)):
                    h = 2 * p + hh
                    kt, _, col, q0, q1 = tile_of(p, hh, r)
                    pe.matmul(ps[:, col:col + q1 - q0], k_stack[0:ROWS_P, h, P * kt:P * kt + P],
                              q_stack[0:ROWS_P, h, q0:q1], start=(n == 0), stop=False,
                              skip_group_check=True)
                    c, mask = (P * kt - q0, mask_low) if forward(h) else (P * kt - q0, mask_up)
                    ins = pe.matmul(ps[:, col + c:col + c + P], ident_bf, mask, start=False,
                                    stop=True, skip_group_check=True)
                ins.then_inc(*g_full.step("scores", k, p, slot))

            def values(it, k, p):
                for slot in range(5):
                    pe.wait_ge(*exp_hi.at(it, k, p, slot))
                    lo = p_lo_v if slot in LO_ON_VECTOR else p_lo_g
                    pe.wait_ge(*lo.at(it, k, p, slot))
                ps = take(ring_y, it, ("o", k, p), o_step, (k, p, "out"))
                first = True
                for qt in range(NT):
                    for hh in range(2):
                        g = 2 * qt + hh
                        h = 2 * p + hh
                        sees = [r for r in range(NT) if tile_of(p, hh, r)[3] <= P * qt < tile_of(p, hh, r)[4]]
                        for r in sees:
                            kt, slot, col, q0, _ = tile_of(p, hh, r)
                            c = col + P * qt - q0
                            for part in range(2):
                                last = r == sees[-1] and part == 1
                                ins = pe.matmul(ps[:, 64 * g:64 * g + 49],
                                                ps_buf[p % 2][slot][part][:, c:c + P],
                                                v_parts[k % 2][:, kt, h, 0:49], start=first,
                                                stop=last, skip_group_check=True)
                                first = False
                ins.then_inc(*y_full.step("o", k, p))

            def stage_att(it, k):
                for p in range(NPAIR + 3):
                    if p in (0, NPAIR // 2):
                        for what in ("q", "k"):
                            pe.wait_ge(*scattered[what, p // (NPAIR // 2)].at(it, k, 5))
                    if 1 <= p <= NPAIR:
                        pe.wait_ge(*shift_step.at(it, k, p - 1, 1))
                        ps = take(ring_u, it, ("shift", k, p - 1), shift_out, (k, p - 1))
                        pe.transpose(ps[0:16, 0:P // 2].bitcast(BF16),
                                     shift[(p - 1) % 2][:, :, :].rearrange("p c g -> p (c g)"), ident_bf
                                     ).then_inc(*u_full.step("shift", k, p - 1))
                    if 2 <= p < NPAIR + 2:
                        pe.wait_ge(*shift_row[p % 2].at(it, k, p - 2))
                    for i in range(8):
                        if p < NPAIR:
                            score(it, k, p, i)
                        if i < 5 and 2 <= p < NPAIR + 2:
                            score_t(it, k, p - 2, i)
                    if p >= 3:
                        if p == 3:
                            pe.wait_ge(*v_step.at(it, k, 1, "third"))
                        values(it, k, p - 3)
                    if p < 2:
                        tail(it, k - 1, p)
                    if p in ATT_AT:
                        prep[ATT_AT[p]](it, prep_stage(k))

            def flush(it, k):
                tail(it, k, 0)
                tail(it, k, 1)

            def setup():
                pe.wait_ge(w_lo_done, 17)
                pe.wait_ge(w_hi_done, 15)
                pe.wait_ge(aug_in, 32)
                pe.wait_ge(ones_done, 3)

            program(pe, (u_full, g_full, y_full, h_used), stage_ffn, stage_att, prep, flush, setup)

        @block.scalar
        def _(act):
            xs = a["L0_attn_x"].rearrange("(i s) (t p) d -> i s p t d", s=2, p=P)
            os = out.rearrange("(i s) (t p) d -> i s p t d", s=2, p=P)

            def load(it, s):
                act.wait_ge(*x_new.at(it, s, 1))
                act.dma_start(x_in[s][:, :, :], xs[(it + 1) & (ITERS - 1), s]
                              ).then_inc(*x_loaded[s].step(s))

            def store(it, s):
                act.wait_ge(*x_new.at(it, NS - 2 + s, 1))
                act.dma_start(os[it, s], x_tok[s][:, :, :]).then_inc(*stored[s].step(s))

            def hi_part(it, key, k, before=False):
                for d in range(ND):
                    act.wait_ge(*u_full.at(it, key, d))
                    act.activation(act_t[k % 2][:, 0, d, :], ring_u.bank(key, d)[:, :], ACT.Copy
                                   ).then_inc(*act_hi.step(key, d))

            def prep_norm(it, k, before=False):
                pass

            def prep_transpose(it, k, before=False):
                if not before:
                    o = (k - 2) % NS
                    prev = k < 2 and k != 0
                    act.wait_ge(*y_full.at(it, "y", o, 1, prev=prev))
                hi_part(it, ("xn", k), k)

            def qk_split(it, k, m):
                for n, what in enumerate(("q", "k")):
                    slot = (2 * m + n) % 2
                    act.wait_ge(*g_full.at(it, what, k, m))
                    if m == 1:
                        act.wait_ge(*scattered[what, 0].at(it, k, 5))
                    else:
                        before, prev = last_stage(k)
                        act.wait_ge(*scattered[what, 1].at(it, before, 5, prev=prev))
                    act.activation(qk_part[slot][:, 0, :], ring_g.bank(what, k, m)[:, :], ACT.Identity,
                                   bias=bias_qk[:, n, m:m + 1]).then_inc(*qk_first.step(k, what, m))
                for n, what in enumerate(("q", "k")):
                    slot = (2 * m + n) % 2
                    act.wait_ge(*qk_step.at(it, k, what, m))
                    act.activation(qk_part[slot][:, 1, :], qk_rest[slot][:, :], ACT.Copy
                                   ).then_inc(*qk_second.step(k, what, m))

            def prep_a(it, k, before=False):
                if STAGES[k][0] == "ffn":
                    act.wait_ge(*u_full.at(it, "logits", k))
                    if k == 4:
                        act.wait_ge(*qk_third.at(it, 3, "k", 1))
                    act.activation(logit_t[:, :], ring_u.bank("logits", k)[:, :], ACT.Copy
                                   ).then_inc(*logits_out.step(k))
                else:
                    qk_split(it, k, 0)

            def prep_b(it, k, before=False):
                if STAGES[k][0] == "ffn":
                    act.wait_ge(*route_step.at(it, k, "minus_max"))
                    act.activation(rt[:, 1], rt[:, 0], ACT.Exp).then_inc(*route_exp.step(k))
                else:
                    for half in range(2):
                        act.wait_ge(*v_step.at(it, k, half, "bias"))
                        vt = v_tok[:, :, :].rearrange("p t (h d) -> p t h d", d=HD)
                        dst = v_parts[k % 2][:, 2 * half:2 * half + 2, :, :]
                        act.activation(dst[:, :, :, 0:HD], vt, ACT.Copy).then_inc(*v_first.step(k, half))
                        act.wait_ge(*v_step.at(it, k, half, "second"))
                        act.activation(dst[:, :, :, HD:2 * HD], vt, ACT.Copy
                                       ).then_inc(*v_second.step(k, half))

            def prep_c(it, k, before=False):
                if STAGES[k][0] == "ffn":
                    act.wait_ge(*u_full.at(it, "comb", k))
                    act.activation(comb_t[k % 2][:, :],
                                   ring_u.bank("comb", k)[:, 0:S // 2].bitcast(F16), ACT.Copy
                                   ).then_inc(*comb_out.step(k))
                else:
                    qk_split(it, k, 1)

            prep = dict(norm=prep_norm, transpose=prep_transpose, a=prep_a, b=prep_b, c=prep_c)

            def hi_of_h(it, k, j):
                act.wait_ge(*h_step.at(it, k, j, "h"))
                if j >= 3:
                    act.wait_ge(*h_used.at(it, k, j - 3))
                act.activation(hs_buf[j % 3][0], h_buf[j % 2], ACT.Copy).then_inc(*h_hi.step(k, j))

            def tail(it, k, part):
                if k < 0:
                    return
                if STAGES[k][0] == "att" and part == 0:
                    hi_part(it, ("o", k), k)

            def stage_ffn(it, k):
                o = (k - 1) % NS
                if STAGES[o][0] == "att":
                    act.wait_ge(*y_full.at(it, "o", o, NPAIR - 1))
                for j in range(NM):
                    act.wait_ge(*g_full.at(it, "gate", k, j))
                    if j >= 2:
                        act.wait_ge(*h_step.at(it, k, j - 2, "g"))
                    elif STAGES[o][0] == "ffn":
                        act.wait_ge(*h_step.at(it, o, NM - 2 + j, "g", prev=k == 0))
                    act.activation(th_buf[j % 2], ring_g.bank("gate", k, j)[:, :], ACT.Tanh, scale=0.5
                                   ).then_inc(*tanh_done.step(k, j))
                    if j >= 1:
                        if j - 1 < 3 and STAGES[o][0] == "ffn":
                            act.wait_ge(*(y_full.at(it, "y", o, 1, prev=k == 0)
                                          if j - 1 == 0 else
                                          h_used.at(it, o, NM - 2, prev=k == 0)))
                        hi_of_h(it, k, j - 1)
                    if (k, j) == (1, 3):
                        load(it, 0)
                    if (k, j) == (NS - 1, 3):
                        store(it, 0)
                    if j < 2:
                        tail(it, k - 1, j)
                    if j in FFN_AT:
                        prep[FFN_AT[j]](it, prep_stage(k))
                hi_of_h(it, k, NM - 1)

            def stage_att(it, k):
                for p in range(NPAIR + 3):
                    if (k, p) == (2, 3):
                        load(it, 1)
                    if 1 <= p <= NPAIR:
                        q = p - 1
                        act.wait_ge(*u_full.at(it, "shift", k, q))
                        if q >= 2:
                            act.wait_ge(*shift_row[q % 2].at(it, k, q - 2))
                        act.activation(shift_t[q % 2][:, :], ring_u.bank("shift", k, q)[0:16, 0:P // 2]
                                       .bitcast(BF16), ACT.Copy).then_inc(*shift_out.step(k, q))
                        act.wait_ge(*shift_out.at(it, k, q))
                        act.dma_start(q_stack[ROWS_S:ROWS_P, 2 * q:2 * q + 2, :], shift_t[q % 2][:, :]
                                      ).then_inc(*shift_row[q % 2].step(k, q))
                    if 2 <= p < NPAIR + 2:
                        q = p - 2
                        for slot in range(5):
                            n = 5 * q + slot
                            act.wait_ge(*g_full.at(it, "scores", k, q, slot))
                            if n == 0:
                                act.wait_ge(*y_full.at(it, "y", k - 1, 1) if STAGES[k - 1][0] == "ffn"
                                            else y_full.at(it, "o", k - 1, NPAIR - 1))
                            if n >= 2:
                                oq, oslot = divmod(n - 2, 5)
                                lo = p_lo_v if oslot in LO_ON_VECTOR else p_lo_g
                                act.wait_ge(*lo.at(it, k, oq, oslot))
                            src = ring_g.bank("scores", k, q, slot)[:, :]
                            act.activation(p_buf[n % 2], src, ACT.Exp).then_inc(*exp_done.step(k, q, slot))
                            if slot == 0 and q >= 2:
                                act.wait_ge(*y_full.at(it, "o", k, q - 2))
                            act.activation(ps_buf[q % 2][slot][0], src, ACT.Exp
                                           ).then_inc(*exp_hi.step(k, q, slot))
                    if p < 2:
                        tail(it, k - 1, p)
                    if p in ATT_AT:
                        prep[ATT_AT[p]](it, prep_stage(k))

            def flush(it, k):
                store(it, 1)

            def setup():
                for i in range(6):
                    act.wait_ge(raw_in[i], 32 if i < 5 else 16)
                    act.activation(piece(i)[0], raw(i), ACT.Copy).then_inc(w_hi_done, 1)
                act.wait_ge(raw_in[6], 16 * 4)
                for w in range(4):
                    for d in range(ND):
                        act.activation(att_dst(0, w, d), att_src(w, d), ACT.Copy,
                                       scale=0.25 if w == 0 else 1.0).then_inc(w_hi_done, 1)

            for s in range(2):
                act.dma_start(x_in[s][:, :, :], xs[0, s]).then_inc(*x_loaded[s].step(s))
            act.wait_ge(const_in, 16 * N_CONST)
            act.wait_ge(filled, 1)
            act.activation(w_route[:, :, 0:E], raw_route, ACT.Copy).then_inc(w_hi_done, 1)
            program(act, (tanh_done, h_hi, act_hi, logits_out, route_exp, comb_out, qk_first, qk_second,
                          v_first, v_second, exp_done, exp_hi, shift_out, *shift_row, *x_loaded,
                          *stored), stage_ffn, stage_att, prep, flush, setup)
            for s in range(2):
                act.wait_ge(*stored[s].at(ITERS - 1, s))
                act.wait_ge(*x_loaded[s].at(ITERS - 1, s))

        @block.vector
        def _(dve):
            def lo_part(it, key, k):
                for d in range(ND):
                    dve.wait_ge(*act_hi.at(it, key, d))
                    dve.tensor_tensor(act_t[k % 2][:, 1, d, :], ring_u.bank(key, d)[:, :],
                                      act_t[k % 2][:, 0, d, :].bitcast(F32), ALU.subtract
                                      ).then_inc(*act_lo.step(key, d))

            def prep_norm(it, k, before=False):
                s = STAGES[k][1]
                x = x_in[s] if k < 2 else x_tok[s]
                if k < 2:
                    dve.wait_ge(*x_loaded[s].at(it, s, prev=k == 1))
                else:
                    dve.wait_ge(*x_new.at(it, k - 2, 1))
                for t in range(NT):
                    dve.bn_stats(stats[:, t, :], x[:, t, :]).then_inc(*norm_step.step(k, "stats", t))
                dve.wait_ge(*norm_step.at(it, k, "stats", NT - 1))
                even_mean, even_var, odd_mean, odd_var = (stats[:, :, c] for c in (1, 2, 4, 5))
                dve.tensor_tensor(mom[:, 0, :], even_mean, odd_mean, ALU.add
                                  ).then_inc(*norm_step.step(k, "means"))
                dve.tensor_tensor(mom[:, 1, :], even_mean, odd_mean, ALU.subtract
                                  ).then_inc(*norm_step.step(k, "apart"))
                dve.tensor_tensor(mom[:, 2, :], even_var, odd_var, ALU.add
                                  ).then_inc(*norm_step.step(k, "within"))
                dve.wait_ge(*norm_step.at(it, k, "apart"))
                dve.tensor_tensor(mom[:, 3, :], mom[:, 1, :], mom[:, 1, :], ALU.mult
                                  ).then_inc(*norm_step.step(k, "square"))
                dve.wait_ge(*norm_step.at(it, k, "within"))
                dve.tensor_scalar(mom[:, 4, :], mom[:, 2, :], 1.0 / D, EPS, ALU.mult, ALU.add
                                  ).then_inc(*norm_step.step(k, "scaled"))
                dve.tensor_scalar(mean[:, :], mom[:, 0, :], 0.5, None, ALU.mult
                                  ).then_inc(*norm_step.step(k, "mean"))
                dve.wait_ge(*norm_step.at(it, k, "scaled"))
                dve.scalar_tensor_tensor(var_eps[:, :], mom[:, 3, :], 0.25, mom[:, 4, :], ALU.mult,
                                         ALU.add).then_inc(*norm_step.step(k, "eps"))
                dve.wait_ge(*rstd_done.at(it, k))
                if not before:
                    dve.wait_ge(*u_full.at(it, ("xn", (k - 1) % NS), ND - 1, prev=k == 1))
                for t in range(NT):
                    dve.tensor_scalar(xn_tok[:, t, :], x[:, t, :], mean[:, t:t + 1], rstd[:, t:t + 1],
                                      ALU.subtract, ALU.mult).then_inc(*norm_step.step(k, "apply", t))

            def prep_transpose(it, k, before=False):
                lo_part(it, ("xn", k), k)

            def qk_rests(it, k, m):
                for n, what in enumerate(("q", "k")):
                    slot = (2 * m + n) % 2
                    dve.wait_ge(*qk_first.at(it, k, what, m))
                    if m == 1:
                        dve.wait_ge(*qk_third.at(it, k, what, 0))
                        dve.wait_ge(*v_step.at(it, k, 1, "third"))
                    else:
                        before, prev = last_stage(k)
                        dve.wait_ge(*qk_third.at(it, before, what, 1, prev=prev))
                        dve.wait_ge(*qk_second.at(it, before, what, 1, prev=prev))
                    dve.scalar_tensor_tensor(qk_rest[slot][:, :], ring_g.bank(what, k, m)[:, :],
                                             bias_qk[:, n, m:m + 1], qk_part[slot][:, 0, :],
                                             ALU.add, ALU.subtract).then_inc(*qk_step.step(k, what, m))

            def prep_a(it, k, before=False):
                if STAGES[k][0] == "att":
                    qk_rests(it, k, 0)

            def prep_b(it, k, before=False):
                if STAGES[k][0] == "ffn":
                    route(it, k)
                else:
                    for half in range(2):
                        dve.wait_ge(*g_full.at(it, "v", k, half))
                        if half:
                            dve.wait_ge(*v_step.at(it, k, 0, "third"))
                        else:
                            dve.wait_ge(*qk_third.at(it, k, "q", 0))
                        flat = v_tok[:, :, :]
                        vt = flat.rearrange("p t (h d) -> p t h d", d=HD)
                        dst = v_parts[k % 2][:, 2 * half:2 * half + 2, :, :]
                        dve.tensor_tensor(flat, ring_g.bank("v", k, half)[:, :].rearrange(
                            "p (t d) -> p t d", d=D), bias_v[:, :].unsqueeze(1).broadcast_to((P, 2, D)),
                            ALU.add).then_inc(*v_step.step(k, half, "bias"))
                        dve.wait_ge(*v_first.at(it, k, half))
                        dve.tensor_tensor(vt, vt, dst[:, :, :, 0:HD], ALU.subtract
                                          ).then_inc(*v_step.step(k, half, "second"))
                        dve.wait_ge(*v_second.at(it, k, half))
                        dve.tensor_tensor(dst[:, :, :, 2 * HD:3 * HD], vt, dst[:, :, :, HD:2 * HD],
                                          ALU.subtract).then_inc(*v_step.step(k, half, "third"))

            def route(it, k):
                def done(name, ins):
                    ins.then_inc(*route_step.step(k, name))
                    dve.wait_ge(*route_step.at(it, k, name))

                d, e, pick, sel, tmp, one = (rt[:, i] for i in range(6))

                def wide(i):
                    return top[:, i, :].unsqueeze(2).broadcast_to((P, NT, E))

                dve.wait_ge(*u_full.at(it, "route", k))
                done("sum", dve.tensor_reduce(logit[:, :, :], ring_u.bank("route", k)[:, :]
                     .rearrange("p (t m) -> p t m", m=P)[:, :, 0:2 * E]
                     .rearrange("p t (c e) -> p t e c", e=E), X, ALU.add))
                done("max", dve.tensor_reduce(top[:, 0, :], logit[:, :, :], X, ALU.max))
                done("minus_max", dve.tensor_tensor(d, logit[:, :, :], wide(0), ALU.subtract))
                done("hit1", dve.scalar_tensor_tensor(pick, d, 0.0, rev, ALU.is_ge, ALU.mult))
                done("low1", dve.tensor_reduce(top[:, 1, :], pick, X, ALU.max))
                done("one1", dve.tensor_tensor(sel, pick, wide(1), ALU.is_equal))
                done("rest", dve.scalar_tensor_tensor(tmp, sel, -BIG, d, ALU.mult, ALU.add))
                done("max2", dve.tensor_reduce(top[:, 2, :], tmp, X, ALU.max))
                done("hit2", dve.tensor_tensor(pick, tmp, wide(2), ALU.is_equal))
                done("rev2", dve.tensor_tensor(pick, pick, rev, ALU.mult))
                done("low2", dve.tensor_reduce(top[:, 3, :], pick, X, ALU.max))
                done("one2", dve.tensor_tensor(one, pick, wide(3), ALU.is_equal))
                done("both", dve.tensor_tensor(sel, sel, one, ALU.add))
                dve.wait_ge(*route_exp.at(it, k))
                done("chosen", dve.tensor_tensor(tmp, sel, e, ALU.mult))
                done("sum2", dve.tensor_reduce(top[:, 4, :], tmp, X, ALU.add))
                done("sum16", dve.tensor_reduce(top[:, 5, :], e, X, ALU.add))
                done("den", dve.scalar_tensor_tensor(top[:, 6, :], top[:, 5, :], 1e-9, top[:, 4, :],
                                                     ALU.mult, ALU.add))
                done("rden", dve.reciprocal(top[:, 7, :], top[:, 6, :]))
                done("comb", dve.tensor_tensor(one, tmp, wide(7), ALU.mult))
                done("hi", dve.tensor_copy(comb[:, :, 0:E], one))
                done("lo", dve.tensor_tensor(comb[:, :, E:2 * E], one, comb[:, :, 0:E], ALU.subtract))

            def prep_c(it, k, before=False):
                if STAGES[k][0] == "att":
                    qk_rests(it, k, 1)

            prep = dict(norm=prep_norm, transpose=prep_transpose, a=prep_a, b=prep_b, c=prep_c)

            def update(it, k):
                s = STAGES[k][1]
                for half in range(2):
                    dve.wait_ge(*y_full.at(it, "y", k, half))
                    xs = x_tok[s][:, 2 * half:2 * half + 2, :]
                    y = ring_y.bank("y", k, half)[:, :].rearrange("p (t d) -> p t d", d=D)
                    if STAGES[k][0] == "att":
                        if half == 0:
                            dve.wait_ge(*bias_added.at(it, k))
                        ins = dve.tensor_tensor(xs, y, xs, ALU.add)
                    else:
                        if k < 2 and half == 0:
                            dve.wait_ge(*stored[s].at(it, s, prev=True))
                        x = x_in[s][:, 2 * half:2 * half + 2, :] if k < 2 else xs
                        ins = dve.scalar_tensor_tensor(xs, y, 0.25, x, ALU.mult, ALU.add)
                    ins.then_inc(*x_new.step(k, half))

            def tail(it, k, part):
                if k < 0:
                    return
                if STAGES[k][0] == "att" and part == 0:
                    lo_part(it, ("o", k), k)
                if part == 1:
                    update(it, k)

            def stage_ffn(it, k):
                o = (k - 1) % NS
                for j in range(NM):
                    dve.wait_ge(*tanh_done.at(it, k, j))
                    if j >= 2:
                        dve.wait_ge(*h_hi.at(it, k, j - 2))
                        dve.wait_ge(*h_lo.at(it, k, j - 2))
                    elif STAGES[o][0] == "ffn":
                        dve.wait_ge(*h_hi.at(it, o, NM - 2 + j, prev=k == 0))
                        dve.wait_ge(*h_lo.at(it, o, NM - 2 + j, prev=k == 0))
                    h = h_buf[j % 2]
                    dve.scalar_tensor_tensor(h, th_buf[j % 2], 1.0, ring_g.bank("gate", k, j)[:, :],
                                             ALU.add, ALU.mult).then_inc(*h_step.step(k, j, "g"))
                    dve.wait_ge(*h_step.at(it, k, j, "g"))
                    dve.wait_ge(*u_full.at(it, "up", k, j))
                    ins = dve.tensor_tensor(h, ring_u.bank("up", k, j)[:, :], h, ALU.mult)
                    ins.then_inc(*h_step.step(k, j, "u" if j >= NSH else "h"))
                    if j >= NSH:
                        dve.wait_ge(*h_step.at(it, k, j, "u"))
                        dve.wait_ge(*u_full.at(it, "weight", k, j))
                        dve.tensor_tensor(h, ring_u.bank("weight", k, j)[:, :], h, ALU.mult
                                          ).then_inc(*h_step.step(k, j, "h"))
                    if j < 2:
                        tail(it, k - 1, j)
                    if j in FFN_AT:
                        prep[FFN_AT[j]](it, prep_stage(k))

            def stage_att(it, k):
                for p in range(NPAIR + 3):
                    for i in range(8):
                        if p < NPAIR:
                            h, qt = 2 * p + i // NT, i % NT
                            k0, k1 = keys(h, qt)
                            dve.wait_ge(*u_full.at(it, "max", k, p, i))
                            if i == 0 and p >= 2:
                                dve.wait_ge(*shift_step.at(it, k, p - 2, 1))
                            dve.tensor_reduce(row_max[p % 2][:, i:i + 1],
                                              ring_u.bank("max", k, p, i)[:, 0:k1 - k0], X, ALU.max
                                              ).then_inc(*max_done.step(k, p, i))
                        if i in LO_ON_VECTOR and 2 <= p < NPAIR + 2:
                            q = p - 2
                            dve.wait_ge(*exp_hi.at(it, k, q, i))
                            dve.tensor_tensor(ps_buf[q % 2][i][1], p_buf[(5 * q + i) % 2],
                                              ps_buf[q % 2][i][0], ALU.subtract
                                              ).then_inc(*p_lo_v.step(k, q, i))
                    if p < NPAIR:
                        dve.wait_ge(*max_done.at(it, k, p, 7))
                        if p >= 2:
                            dve.wait_ge(*u_full.at(it, "shift", k, p - 2))
                        dve.tensor_scalar(shift[p % 2][:, 0, :], row_max[p % 2][:, :], -1.0, None, ALU.mult
                                          ).then_inc(*shift_step.step(k, p, 0))
                        dve.wait_ge(*shift_step.at(it, k, p, 0))
                        dve.scalar_tensor_tensor(shift[p % 2][:, 1, :], row_max[p % 2][:, :], -1.0,
                                                 shift[p % 2][:, 0, :], ALU.mult, ALU.subtract
                                                 ).then_inc(*shift_step.step(k, p, 1))
                    if p >= 3:
                        q = p - 3
                        dve.wait_ge(*y_full.at(it, "o", k, q))
                        if q >= 1:
                            dve.wait_ge(*o_step.at(it, k, q - 1, "out"))
                        elif k == 3:
                            dve.wait_ge(*u_full.at(it, ("o", 2), ND - 1))
                        ps = ring_y.bank("o", k, q)[:, :].rearrange("p (g c) -> p g c", c=64)
                        dve.tensor_reduce(o_sum[:, :, :], ps[:, :, 0:3 * HD].rearrange(
                            "p g (c d) -> p g d c", c=PARTS), X, ALU.add).then_inc(*o_step.step(k, q, "sum"))
                        dve.reciprocal(o_rden[:, :], ps[:, :, 3 * HD]).then_inc(*o_step.step(k, q, "rden"))
                        dve.wait_ge(*o_step.at(it, k, q, "rden"))
                        dve.tensor_tensor(
                            o_tok[:, :, 2 * HD * q:2 * HD * q + 2 * HD].rearrange("p t (h d) -> p t h d", h=2),
                            o_sum[:, :, :].rearrange("p (t h) d -> p t h d", h=2),
                            o_rden[:, :].rearrange("p (t h) -> p t h", h=2).unsqueeze(3)
                            .broadcast_to((P, NT, 2, HD)), ALU.mult).then_inc(*o_step.step(k, q, "out"))
                    if p < 2:
                        tail(it, k - 1, p)
                    if p in ATT_AT:
                        prep[ATT_AT[p]](it, prep_stage(k))

            def flush(it, k):
                update(it, k)

            def setup():
                for i in range(6):
                    dve.wait_ge(w_hi_done, i + 2)
                    dve.tensor_tensor(piece(i)[1], raw(i), piece(i)[0].bitcast(F32), ALU.subtract
                                      ).then_inc(w_lo_done, 1)
                for n in range(4 * ND):
                    w, d = divmod(n, ND)
                    dve.wait_ge(w_hi_done, n + 8)
                    if w == 0:
                        for m in range(ND):
                            ins = dve.scalar_tensor_tensor(
                                att_dst(1, w, d)[:, m], att_src(w, d)[:, m], 0.25,
                                att_dst(0, w, d)[:, m].bitcast(F32), ALU.mult, ALU.subtract)
                    else:
                        ins = dve.tensor_tensor(att_dst(1, w, d), att_src(w, d),
                                                att_dst(0, w, d).bitcast(F32), ALU.subtract)
                    ins.then_inc(w_lo_done, 1)

            dve.memset(w_route[:, :, :].bitcast(F32), 0.0).then_inc(filled, 1)
            dve.memset(comb[:, :, :], 0.0).then_inc(filled, 1)
            dve.wait_ge(filled, 2)
            dve.wait_ge(const_in, 16 * N_CONST)
            dve.tensor_scalar(bias_qk[:, 0, :], bias_qk[:, 0, :], 0.25, None, ALU.mult).then_inc(w_lo_done, 1)
            dve.wait_ge(w_hi_done, 1)
            dve.tensor_tensor(w_route[:, :, E:2 * E], raw_route, w_route[:, :, 0:E].bitcast(F32),
                              ALU.subtract).then_inc(w_lo_done, 2)
            dve.wait_ge(w_lo_done, 3)
            program(dve, (h_step, act_lo, norm_step, route_step, qk_step, v_step, max_done, shift_step,
                          p_lo_v, o_step, x_new), stage_ffn, stage_att, prep, flush, setup)

        @block.gpsimd
        def _(pool):
            def prep_norm(it, k, before=False):
                pool.wait_ge(*norm_step.at(it, k, "eps"))
                pool.tensor_tensor(rstd[:, :], var_eps[:, :], minus_half[:, :], ALU.pow
                                   ).then_inc(*rstd_done.step(k))

            def nothing(it, k, before=False):
                pass

            def thirds(it, k, m):
                for n, what in enumerate(("q", "k")):
                    slot = (2 * m + n) % 2
                    pool.wait_ge(*qk_second.at(it, k, what, m))
                    pool.tensor_tensor(qk_part[slot][:, 2, :], qk_rest[slot][:, :], qk_part[slot][:, 1, :],
                                       ALU.subtract).then_inc(*qk_third.step(k, what, m))

            def prep_a(it, k, before=False):
                if STAGES[k][0] == "att":
                    thirds(it, k, 0)

            def prep_c(it, k, before=False):
                if STAGES[k][0] == "att":
                    thirds(it, k, 1)

            prep = dict(norm=prep_norm, transpose=nothing, a=prep_a, b=nothing, c=prep_c)

            def lo_of_h(it, k, j):
                pool.wait_ge(*h_hi.at(it, k, j))
                pool.tensor_tensor(hs_buf[j % 3][1], h_buf[j % 2], hs_buf[j % 3][0].bitcast(F32),
                                   ALU.subtract).then_inc(*h_lo.step(k, j))

            def stage_ffn(it, k):
                for j in range(NM):
                    if j >= 1:
                        lo_of_h(it, k, j - 1)
                    if j in FFN_AT:
                        prep[FFN_AT[j]](it, prep_stage(k))
                lo_of_h(it, k, NM - 1)

            def stage_att(it, k):
                s = STAGES[k][1]
                for p in range(NPAIR + 3):
                    if p == 0:
                        pool.wait_ge(*norm_step.at(it, k, "apply", NT - 1))
                        pool.tensor_tensor(x_tok[s][:, :, :], x_tok[s][:, :, :],
                                           bias_f[:, :].unsqueeze(1).broadcast_to((P, NT, D)), ALU.add
                                           ).then_inc(*bias_added.step(k))
                    if 2 <= p < NPAIR + 2:
                        q = p - 2
                        for slot in range(5):
                            if slot not in LO_ON_VECTOR:
                                pool.wait_ge(*exp_hi.at(it, k, q, slot))
                                pool.tensor_tensor(ps_buf[q % 2][slot][1], p_buf[(5 * q + slot) % 2],
                                                   ps_buf[q % 2][slot][0], ALU.subtract
                                                   ).then_inc(*p_lo_g.step(k, q, slot))
                    if p in ATT_AT:
                        prep[ATT_AT[p]](it, prep_stage(k))

            def flush(it, k):
                pass

            pool.memset(minus_half[:, :], -0.5).then_inc(ones_done, 1)
            for v in v_parts:
                pool.memset(v[:, :, :, 3 * HD:VW], 1.0).then_inc(ones_done, 1)
            pool.wait_ge(ones_done, 3)
            program(pool, (rstd_done, h_lo, qk_third, p_lo_g, bias_added),
                    stage_ffn, stage_att, prep, flush)


_INS = ["L0_attn_x", "L0_attn_Wq", "L0_attn_bq", "L0_attn_Wk", "L0_attn_bk", "L0_attn_Wv", "L0_attn_bv",
        "L0_attn_Wf", "L0_attn_bf", "L0_ffn_router_w", "L0_ffn_wg_r", "L0_ffn_wu_r", "L0_ffn_wd_r",
        "L0_ffn_wg_s", "L0_ffn_wu_s", "L0_ffn_wd_s"]


def constants():
    import numpy as np

    bf16 = mybir.dt.np(BF16)
    eye = np.eye(P, dtype=np.float32)
    rev = np.tile(np.arange(E, 0, -1, dtype=np.float32), NT)
    c32 = np.concatenate([eye, np.broadcast_to(rev, (P, NT * E))], 1)
    select = np.zeros((P, 8, P), np.float32)
    for j in range(8):
        for m in range(P):
            for c in range(2):
                select[c * E + 2 * j + m // ME, j, m] = 1.0
    c16 = np.concatenate([eye, select.reshape(P, -1)], 1).astype(np.float16)
    neg = np.float32(-1e9)
    cbf = np.concatenate([eye, np.triu(np.full((P, P), neg), 1), np.tril(np.full((P, P), neg), -1)],
                         1).astype(bf16)
    half = H // 2
    base = np.float32(24.0 ** (1.0 / half))
    slopes = (np.float32(1.0) / base ** np.arange(1, half + 1, dtype=np.float32)).astype(np.float32)
    slopes = np.concatenate([slopes, -slopes])
    parts, rest = [], slopes
    for _ in range(PARTS):
        parts.append(rest.astype(bf16))
        rest = rest - parts[-1].astype(np.float32)
    q_rows = np.broadcast_to(np.stack(parts)[:, :, None], (PARTS, H, S))
    pos = np.broadcast_to((np.arange(S) - S // 2).astype(np.float32), (PARTS, H, S))
    k_rows = np.concatenate([pos, np.ones((2, H, S), np.float32)]).astype(bf16)
    return {"c32": c32.astype(np.float32), "c16": c16, "cbf": cbf,
            "q_rows": np.ascontiguousarray(q_rows), "k_rows": k_rows}


def kernel(**inputs):
    import numpy as _np
    import concourse.bacc as _bacc
    from concourse import mybir as _mybir
    from concourse.bass_utils import run_bass_kernel_spmd as _run

    arrays = {n: _np.ascontiguousarray(inputs[n]) for n in _INS}
    arrays.update(constants())
    book = Book()
    for final in (False, True):
        book.final = final
        nc = _bacc.Bacc("TRN2", target_bir_lowering=False, num_devices=1)
        aps = {n: nc.dram_tensor(f"in_{n}", v.shape, _mybir.dt.from_np(v.dtype), kind="ExternalInput").ap()
               for n, v in arrays.items()}
        out = nc.dram_tensor("out_0_dram", (B, S, D), F32, kind="ExternalOutput").ap()
        build(nc, book, aps, out)
    r = _run(nc, [{f"in_{n}": v for n, v in arrays.items()}], core_ids=[0])
    return r.results[0]["out_0_dram"]
```

```python
from contextlib import ExitStack

import concourse.bass as bass
from concourse import mybir

F32 = mybir.dt.float32
F32R = mybir.dt.float32r
BF16 = mybir.dt.bfloat16
F16 = mybir.dt.float16
ALU = mybir.AluOpType
ACT = mybir.ActivationFunctionType
X = mybir.AxisListType.X

P = 128
B, S, D = 16, 512, 256
H, HD = 16, 16
NT = S // P
ND = D // P
E = 16
ME, MS = 64, 128
NM = 10
NSH = 2
ITERS = B // 2 - 1
NPAIR = H // 2
HB = P // HD
PARTS = 3
ROWS_S = 6 * HD + 3
ROWS_P = ROWS_S + 2
QB = (0, 0, 0, 1, 1, 2)
KB = (0, 1, 2, 0, 1, 0)
EPS = 1e-5
BIG = 1e30
N_CONST = 4
N_BIAS = 6
N_ONES = 4
VW = 3 * HD + 1
NPS = 4
LAG = NPS - 1

PERIOD = 2 * NM
STEPS = 2 * PERIOD
FIRST = STEPS - 5
ATT = 4
MID, END = 0, 1
PREP_AT = {0: [("b3", "first", END)], 1: [("c", "first", END)], 2: [("moments", "second", END)],
           3: [("norm", "second", END)], 4: [("transpose", "second", MID)],
           5: [("a", "second", MID)], 6: [("b", "second", MID)], 7: [("b2", "second", END)],
           8: [("b3", "second", END)], 9: [("c", "second", MID)],
           11: [("moments", "att n", END)], 12: [("norm", "att n", END)],
           13: [("transpose", "att n", MID), ("a", "att n", END)], 14: [("b", "att n", END)],
           15: [("c", "att n", END), ("moments", "first n", END)],
           16: [("norm", "first n", END)], 17: [("transpose", "first n", MID), ("a", "first n", END)],
           18: [("b", "first n", MID)], 19: [("b2", "first n", END)]}


def phase(it):
    return "loop" if not isinstance(it, int) else "before" if it < 0 else "after"


def attends(it, q):
    return phase(it) == "loop" or (it, q) in ((-1, 1), (ITERS, 0))


def attended(it, q):
    return phase(it) == "loop" or (it == ITERS and q < 2)


def first_time(it, i, at):
    return phase(it) == "before" and (it, i) == (-1, at)


def preparation(it, step, at):
    q, f = divmod(step, PERIOD)
    pieces = []
    for piece, what, place in PREP_AT.get(f, ()):
        left_out = {"loop": False, "after": phase(it) == "after" and (what != "second" or it > ITERS),
                    "before": phase(it) == "before" and what != "first n" and (what == "second" or it < -1)
                    }[phase(it)]
        if left_out or place != at:
            continue
        to = 1 - q if what.endswith("n") else q
        pieces.append((piece, {"first": 2 * to, "second": 2 * to + 1}.get(what.split()[0], ATT + to)))
    return pieces


def there(it, tile):
    first = tile % PERIOD < NM
    return {"before": phase(it) == "before" and it == -1 and tile >= 0 and first, "loop": True,
            "after": tile < 0 or (phase(it) == "after" and it == ITERS and not first)}[phase(it)]


class Book:

    def __init__(self):
        self.events = {}
        self.peeled = {}
        self.slots = {}
        self.final = False


class Signal:

    def __init__(self, ctx, nc, book, name, unit=1):
        self.sem = ctx.enter_context(nc.semaphore(name))
        self.name, self.unit, self.book = name, unit, book
        if not book.final:
            book.events[name], book.peeled[name] = {}, set()
        self.events, self.peeled = book.events[name], book.peeled[name]
        self.value = 0

    def step(self, it, *key):
        if isinstance(it, int):
            self.peeled.add((it, key))
            if self.unit > 1 or not self.book.final:
                self.value += self.unit
                return self.sem, self.unit
            to = (it + 2) * len(self.events) + self.events[key] + 1
            assert to > self.value, (self.name, key, to, self.value)
            by, self.value = to - self.value, to
            return self.sem, by
        if not self.book.final:
            assert key not in self.events, (self.name, key)
            self.events[key] = len(self.events)
        return self.sem, self.unit

    def at(self, it, *key, prev=False):
        if not self.book.final:
            return self.sem, 1
        n, i = len(self.events), self.events[key]
        it = it - 1 if prev else it
        if phase(it) != "loop" and it != ITERS - 1 and (it, key) not in self.peeled:
            return (self.sem, (ITERS + 2) * n * self.unit) if it > 0 else None
        return self.sem, (it + 2) * (n * self.unit) + (i + 1) * self.unit

    def pass_over(self, eng, it, *key):
        if self.book.final and phase(it) != "loop":
            gap = ((it + 2) * len(self.events) + self.events[key]) * self.unit - self.value
            if gap > 0:
                eng.sem_inc(self.sem, gap)
                self.value += gap

    def enter_loop(self, eng):
        rest = 2 * len(self.events) * self.unit - self.value
        if rest > 0:
            eng.sem_inc(self.sem, rest)
        self.value = (ITERS + 2) * len(self.events) * self.unit

    def entered(self):
        return self.sem, max(2 * len(self.events), 1) * self.unit


class Ring:

    def __init__(self, book, name, banks):
        self.book, self.banks = book, banks
        if not book.final:
            book.slots[name] = []
        self.slots = book.slots[name]
        self.last = {}
        self.order = {key: i for i, (key, _, _, _) in enumerate(self.slots)}

    def bank(self, *key):
        return self.banks[self.order.get(key, 0) % len(self.banks)]

    def take(self, it, key, freed, freed_key, late=False):
        nb = len(self.banks)
        if not self.book.final:
            if not isinstance(it, int):
                self.slots.append((key, freed.name, freed_key, late))
            return None
        i = self.order[key]
        if isinstance(it, int):
            tenant = self.last.get((phase(it), i % nb))
            self.last[phase(it), i % nb] = (freed, freed_key, it + late)
            if tenant:
                return tenant[0].at(tenant[2], *tenant[1])
            if it < 0:
                return None
            i = i % nb
        n = -(-len(self.slots) // nb) * nb
        i -= nb
        while i % n >= len(self.slots):
            i -= nb
        _, name, k, late = self.slots[i % n]
        return self.signals[name].at(it, *k, prev=i < 0 and not late)


def build(nc, book, a, out):
    ctx = ExitStack()
    with ctx:
        def sb(name, shape, dt=F32):
            return ctx.enter_context(nc.sbuf_tensor(name, shape, dt))

        sigs = {}

        def signal(name, unit=1):
            sigs[name] = Signal(ctx, nc, book, name, unit)
            return sigs[name]

        def sem(name):
            return ctx.enter_context(nc.semaphore(name))

        bank = [ctx.enter_context(nc.psum_tensor(f"bank{i}", [P, 512], F32)) for i in range(8)]
        ring_u = Ring(book, "u", bank[0:3])
        ring_g = Ring(book, "g", bank[3:5])
        ring_y = Ring(book, "y", bank[5:7])
        ring_o = Ring(book, "o", bank[7:8])

        w_gate = sb("w_gate", [P, 2, ND, NM * P], F32R)
        w_up = sb("w_up", [P, 2, ND, NM * P], F32R)
        w_down = sb("w_down", [P, 2, NM, D], F32R)
        w_attn = sb("w_attn", [P, 2, 4, ND, D], F32R)
        w_route = sb("w_route", [P, ND, P], F32R)
        x_in = sb("x_in", [P, NT, D])
        x_mid = [sb(f"x_mid{s}", [P, NT, D]) for s in range(2)]
        x_out = [sb(f"x_out{s}", [P, NT, D]) for s in range(2)]
        xn_tok = sb("xn_tok", [P, NT, D])
        o_tok = sb("o_tok", [P, NT, D])
        act_t = [sb(f"act_t{i}", [P, 2, ND, S], F32R) for i in range(2)]
        q_stack = sb("q_stack", [P, H, S], BF16)
        k_stack = sb("k_stack", [P, H, S], BF16)
        v_parts = [sb(f"v_parts{i}", [P, NT, H, VW], BF16) for i in range(2)]
        th_buf = sb("th_buf", [P, S])
        h_buf = [sb(f"h_buf{i}", [P, S])[:, :] for i in range(2)]
        hs_buf = [[sb(f"hs_buf{i}{c}", [P, S], F32R)[:, :] for c in range(2)] for i in range(2)]
        work = sb("work", [P, 2 * S + NPS * S])
        p_buf = [work[:, S * i:S * (i + 1)] for i in range(2)]
        ps_buf = [[work[:, 2 * S + S // 2 * (2 * i + c):2 * S + S // 2 * (2 * i + c + 1)].bitcast(F16)
                   for c in range(2)] for i in range(NPS)]
        stats = sb("stats", [P, NT, 6])
        mom = sb("mom", [P, 5, NT])
        mean = sb("mean", [P, NT])
        var_eps = sb("var_eps", [P, NT])
        rstd = sb("rstd", [P, NT])
        minus_half = sb("minus_half", [P, NT])
        top = sb("top", [P, 8, NT])
        comb = sb("comb", [P, NT, P], F16)
        comb_t = [sb(f"comb_t{i}", [P, S], F16) for i in range(2)]
        qk_part = [sb(f"qk_part{i}", [P, PARTS, S], BF16) for i in range(2)]
        rest = [xn_tok[:, 2 * i:2 * i + 2, :].rearrange("p t d -> p (t d)") for i in range(2)]
        logit_t = rest[1]
        rt = rest[0][:, 0:6 * NT * E].rearrange("p (i t e) -> p i t e", i=6, t=NT)
        logit = rest[0][:, 6 * NT * E:7 * NT * E].rearrange("p (t e) -> p t e", t=NT)
        row_max = [sb(f"row_max{i}", [P, 8]) for i in range(2)]
        shift = [sb(f"shift{i}", [P, 2, 8], BF16) for i in range(2)]
        shift_t = [sb(f"shift_t{i}", [16, P], BF16) for i in range(2)]
        o_sum = sb("o_sum", [P, 8, HD])
        o_rden = sb("o_rden", [P, 8])
        c32 = sb("c32", [P, P + NT * E])
        c16 = sb("c16", [P, P + 8 * P], F16)
        cbf = sb("cbf", [P, 3 * P], BF16)
        bias_qk = sb("bias_qk", [P, 2, ND])
        bias_v = sb("bias_v", [P, D])
        bias_f = sb("bias_f", [P, D])
        ident32, rev = c32[:, 0:P], c32[:, P:].rearrange("p (t e) -> p t e", e=E)
        ident16, select = c16[:, 0:P], c16[:, P:].rearrange("p (j m) -> p j m", m=P)
        ident_bf, mask_up, mask_low = cbf[:, 0:P], cbf[:, P:2 * P], cbf[:, 2 * P:]

        u_full, g_full, y_full = signal("u_full"), signal("g_full"), signal("y_full")
        o_full = signal("o_full")
        h_used = signal("h_used")
        tanh_done, h_hi, act_hi = signal("tanh_done"), signal("h_hi"), signal("act_hi")
        logits_out, route_exp, comb_out = signal("logits_out"), signal("route_exp"), signal("comb_out")
        qk_first, qk_second = signal("qk_first"), signal("qk_second")
        v_first, v_second = signal("v_first"), signal("v_second")
        exp_done, exp_hi, shift_out = signal("exp_done"), signal("exp_hi"), signal("shift_out")
        h_step, act_lo, norm_step = signal("h_step"), signal("act_lo"), signal("norm_step")
        route_step, qk_step, v_step = signal("route_step"), signal("qk_step"), signal("v_step")
        max_done, shift_step = signal("max_done"), signal("shift_step")
        o_step, x_new = signal("o_step"), signal("x_new")
        rstd_done, h_lo, qk_third = signal("rstd_done"), signal("h_lo"), signal("qk_third")
        p_lo, bias_added = signal("p_lo"), signal("bias_added")
        x_loaded = [signal(f"x_loaded{s}", 16) for s in range(2)]
        stored = [signal(f"stored{s}", 16) for s in range(2)]
        scattered = {(att, w, m): signal(f"scattered{att}_{w}{m}", 16)
                     for att in (ATT, ATT + 1) for m in range(2) for w in ("q", "k")}
        shift_row = [signal(f"shift_row{i}", 16) for i in range(2)]
        for r in (ring_u, ring_g, ring_y, ring_o):
            r.signals = sigs
        stack_free = sem("stack_free")
        const_in, bias_in, aug_in = sem("const_in"), sem("bias_in"), sem("aug_in")
        raw_in = [sem(f"raw_in{i}") for i in range(7)]
        filled, w_hi_done, w_lo_done = sem("filled"), sem("w_hi_done"), sem("w_lo_done")
        ones_done = sem("ones_done")

        raw_att = work[:, 0:4 * ND * D].rearrange("p (w k n) -> p w k n", w=4, k=ND)
        raw_route = work[:, 4 * ND * D:4 * ND * D + ND * E].rearrange("p (k e) -> p k e", e=E)

        HALF = NM * P

        def piece_of(i):
            if i < 4:
                w = (w_gate, w_up)[i // 2]
                return w[:, 0, i % 2, :], w[:, 1, i % 2, :]
            half = slice(5 * (i - 4), 5 * (i - 4) + 5)
            return (w_down[:, 0, half, :].rearrange("p j n -> p (j n)"),
                    w_down[:, 1, half, :].rearrange("p j n -> p (j n)"))

        def raw(i):
            t = (q_stack, k_stack)[i // 3]
            flat = t[:, :, :].rearrange("p h s -> p (h s)").bitcast(F32)
            return flat[:, (i % 3) * HALF:(i % 3 + 1) * HALF]

        def att_dst(c, w, k):
            ap = w_attn[:, c, w, k, :]
            return ap.rearrange("p (m d h) -> p m h d", m=ND, h=HB) if w < 2 else \
                ap.rearrange("p (m h d) -> p m h d", m=ND, h=HB)

        def att_src(w, k):
            return raw_att[:, w, k, :].rearrange("p (m h d) -> p m h d", m=ND, h=HB)

        def forward(h):
            return h < H // 2

        def keys(h, qt):
            return (0, P * (qt + 1)) if forward(h) else (P * qt, S)

        def tile_of(pair, hh, r):
            kt = r if forward(2 * pair) else NT - 1 - r
            q0, q1 = (P * kt, S) if forward(2 * pair) else (0, P * (kt + 1))
            slot = {0: 3 * hh, 1: 3 * hh + 1, 2: 2, 3: 3 * hh + 1}[r]
            col = {0: 0, 1: 0, 2: 256 * hh, 3: 384}[r]
            return kt, slot, col, q0, q1

        def slot_tiles(pair, slot):
            return [(hh, r) for hh in range(2) for r in range(NT) if tile_of(pair, hh, r)[1] == slot]

        def row_tile(pair, hh, r):
            return NT - 1 - r if forward(2 * pair) else r

        def act_of(block):
            return act_t[1 if block in (1, 3) else 0]

        def transposed(key, d):
            if key[0] == "o":
                return ring_g, g_full
            return (ring_u, u_full) if d == 0 or key[1] in (0, 2) else (ring_g, g_full)

        def kind(block):
            return "att" if block >= ATT else "ffn"

        def tile(t):
            return divmod(t % (4 * NM), NM)

        def of(signal, it, t, lag, *key):
            return signal.at(it, t % (4 * NM), *key, prev=t + lag < 0)

        def score_items(f):
            if not 3 <= f < 3 + 2 * NPAIR:
                return []
            p, late = divmod(f - 3, 2)
            return [(p, slot) for slot in ((3, 4) if late else (0, 1, 2))]

        def row_items(f):
            p, late = divmod(f, 2)
            return [(p, slot) for slot in ((3, 4) if late else (0, 1, 2))] if p < NPAIR else []

        def item(p, slot):
            return 5 * p + slot

        def before_item(p, slot, by):
            n = item(p, slot) - by
            return divmod(n, 5) if n >= 0 else None

        def program(eng, signals, step, enter=None):
            for i in range(FIRST, STEPS):
                step(-2, i)
            for i in range(STEPS):
                step(-1, i)
            if enter:
                enter()
            for s in signals:
                s.enter_loop(eng)
            with eng.Fori(0, ITERS) as it:
                for i in range(STEPS):
                    step(it, i)
            for i in range(STEPS):
                step(ITERS, i)
            step(ITERS + 1, 0)
            step(ITERS + 1, 1)

        block = ctx.enter_context(nc.Block())

        @block.sync
        def _(sp):
            w = {n.replace("L0_ffn_", ""): ap for n, ap in a.items()}
            for dst, src in ((c32, a["c32"]), (c16, a["c16"]), (cbf, a["cbf"])):
                sp.dma_start(dst[:, :], src).then_inc(const_in, 16)
            sp.dma_start(raw_route, w["router_w"].rearrange("(k p) e -> p k e", p=P)).then_inc(const_in, 16)
            for i in range(6):
                if i < 4:
                    shared = w[("wg_s", "wu_s")[i // 2]][:, P * (i % 2):P * (i % 2) + P, :]
                    routed = w[("wg_r", "wu_r")[i // 2]][:, P * (i % 2):P * (i % 2) + P, :]
                    sp.dma_start(raw(i)[:, 0:NSH * P].rearrange("p (n m) -> p n m", n=NSH),
                                 shared.rearrange("n p m -> p n m")).then_inc(raw_in[i], 16)
                    sp.dma_start(raw(i)[:, NSH * P:].rearrange("p (e m) -> p e m", e=E),
                                 routed.rearrange("e p m -> p e m")).then_inc(raw_in[i], 16)
                else:
                    rows = w["wd_r"].rearrange("(j e) m d -> (e m) j d", e=2)
                    n_sh = NSH if i == 4 else 0
                    j0 = 0 if i == 4 else 5 - NSH
                    if n_sh:
                        sp.dma_start(raw(i)[:, 0:n_sh * D].rearrange("p (n d) -> p n d", n=n_sh),
                                     w["wd_s"].rearrange("n m d -> m n d")).then_inc(raw_in[i], 16)
                    sp.dma_start(raw(i)[:, n_sh * D:].rearrange("p (j d) -> p j d", d=D),
                                 rows[:, j0:j0 + 5 - n_sh, :]).then_inc(raw_in[i], 16)
            for i, n in enumerate(("Wq", "Wk", "Wv", "Wf")):
                sp.dma_start(raw_att[:, i, :, :],
                             a["L0_attn_" + n].rearrange("(k p) n -> p k n", p=P)).then_inc(raw_in[6], 16)
            for i, n in enumerate(("bq", "bk")):
                for m in range(ND):
                    sp.dma_start(bias_qk[:, i, m:m + 1],
                                 a["L0_attn_" + n][P * m:P * m + P].rearrange("(h d) -> d h", h=HB),
                                 allow_slow_non_contiguous=True).then_inc(bias_in, 16)
            for dst, n in ((bias_v, "bv"), (bias_f, "bf")):
                sp.dma_start(dst[:, :], a["L0_attn_" + n].rearrange("(o d) -> o d", o=1)
                             .broadcast_to((P, D))).then_inc(bias_in, 16)
            sp.wait_ge(w_hi_done, 15)
            sp.wait_ge(w_lo_done, 16)
            sp.dma_start(q_stack[6 * HD:ROWS_S, :, :], a["q_rows"]).then_inc(aug_in, 16)
            sp.dma_start(k_stack[6 * HD:ROWS_P, :, :], a["k_rows"]).then_inc(aug_in, 16)
            sp.wait_ge(aug_in, 32)

            def scatter(it, q):
                att = ATT + 1 - q
                for n, (what, m) in enumerate((("q", 0), ("k", 0), ("q", 1), ("k", 1))):
                    if attends(it, q):
                        sp.wait_ge(*g_full.at(it, "scores", ATT + q, 4 * m + 3, 4))
                        sp.sem_inc(stack_free, 1)
                    sp.wait_ge(*qk_third.at(it, att, what, m))
                    stack, parts = (q_stack, QB) if what == "q" else (k_stack, KB)
                    scattered[att, what, m].pass_over(sp, it, 0)
                    for blk in range(6):
                        sp.dma_start(stack[HD * blk:HD * blk + HD, HB * m:HB * m + HB, :],
                                     qk_part[n % 2][:, parts[blk], :]
                                     ).then_inc(*scattered[att, what, m].step(it, blk))

            scatter(-1, 0)
            scatter(-1, 1)
            for s in scattered.values():
                s.enter_loop(sp)
            with sp.Fori(0, ITERS) as it:
                scatter(it, 0)
                scatter(it, 1)
            for event in scattered.values():
                sp.wait_ge(*event.at(ITERS, 5, prev=True))

        @block.tensor
        def _(pe):
            def take(ring, it, key, freed, freed_key, late=False):
                wait = ring.take(it, key, freed, freed_key, late)
                if wait:
                    pe.wait_ge(*wait)
                return ring.bank(*key)

            def product(dst, left, right, first, last):
                pe.matmul(dst, left(0), right(0), start=first, stop=False, skip_group_check=True)
                pe.matmul(dst, left(0), right(1), start=False, stop=False, skip_group_check=True)
                return pe.matmul(dst, left(1), right(0), start=False, stop=last, skip_group_check=True)

            def transpose_act(it, key, src):
                for d in range(ND):
                    ring, full = transposed(key, d)
                    ps = take(ring, it, (key, d), act_lo, (key, d))
                    for t in range(NT):
                        ins = pe.transpose(ps[:, P * t:P * t + P], src[:, t, P * d:P * d + P], ident32)
                    ins.then_inc(*full.step(it, key, d))

            def prepare(it, piece, blk):
                if piece == "transpose":
                    pe.wait_ge(*norm_step.at(it, blk, "apply", NT - 1))
                    transpose_act(it, ("xn", blk), xn_tok)
                elif piece == "a":
                    pe.wait_ge(*act_lo.at(it, ("xn", blk), ND - 1))
                    pe.wait_ge(*act_hi.at(it, ("xn", blk), ND - 1))
                    xt = act_of(blk)
                    if kind(blk) == "att":
                        qk_product(it, blk, 0)
                    else:
                        ps = take(ring_u, it, ("logits", blk), logits_out, (blk,))
                        for d in range(ND):
                            for c in range(2):
                                ins = pe.matmul(ps[:, :], w_route[:, d, :], xt[:, c, d, :],
                                                start=(d + c == 0), stop=(d + c == 2))
                        ins.then_inc(*u_full.step(it, "logits", blk))
                elif piece == "b":
                    if kind(blk) == "att":
                        v_product(it, blk)
                    else:
                        pe.wait_ge(*logits_out.at(it, blk))
                        ps = take(ring_u, it, ("route", blk), route_step, (blk, "sum"))
                        for t in range(NT):
                            ins = pe.transpose(ps[:, P * t:P * t + P], logit_t[:, P * t:P * t + P],
                                               ident32)
                        ins.then_inc(*u_full.step(it, "route", blk))
                elif piece == "c":
                    if kind(blk) == "att":
                        qk_product(it, blk, 1)
                    else:
                        pe.wait_ge(*route_step.at(it, blk, "lo"))
                        ps = take(ring_u, it, ("comb", blk), comb_out, (blk,))
                        ps16 = ps[:, 0:S // 2].bitcast(F16)
                        for t in range(NT):
                            ins = pe.transpose(ps16[:, P * t:P * t + P], comb[:, t, :], ident16)
                        ins.then_inc(*u_full.step(it, "comb", blk))

            def qk_product(it, att, m):
                xt = act_of(att)
                for w, what in enumerate(("q", "k")):
                    ps = take(ring_g, it, (what, att, m), qk_step, (att, what, m))
                    for d in range(ND):
                        ins = product(ps[:, :], lambda c: w_attn[:, c, w, d, P * m:P * m + P],
                                      lambda c: xt[:, c, d, :], d == 0, d == ND - 1)
                    ins.then_inc(*g_full.step(it, what, att, m))

            def token_product(it, ps, half, src, w):
                for i in range(2):
                    t = 2 * half + i
                    for d in range(ND):
                        ins = product(ps[:, D * i:D * i + D], lambda c: src[:, c, d, P * t:P * t + P],
                                      lambda c: w_attn[:, c, w, d, :], i == 0 and d == 0, d == ND - 1)
                return ins

            def v_product(it, att):
                for half in range(2):
                    ps = take(ring_g, it, ("v", att, half), v_step, (att, half, "bias"))
                    token_product(it, ps, half, act_of(att), 2).then_inc(*g_full.step(it, "v", att, half))

            def score(it, att, p, slot):
                ps = take(ring_u, it, ("max", att, p, slot), max_done, (att, p, slot))
                for n, (hh, r) in enumerate(slot_tiles(p, slot)):
                    h, qt, col = 2 * p + hh, row_tile(p, hh, r), tile_of(p, hh, r)[2]
                    k0, k1 = keys(h, qt)
                    pe.matmul(ps[:, col:col + k1 - k0], q_stack[0:ROWS_S, h, P * qt:P * qt + P],
                              k_stack[0:ROWS_S, h, k0:k1], start=(n == 0), stop=False,
                              skip_group_check=True)
                    c, mask = (col + P * qt - k0, mask_up) if forward(h) else (col, mask_low)
                    ins = pe.matmul(ps[:, c:c + P], ident_bf, mask, start=False, stop=True,
                                    skip_group_check=True)
                ins.then_inc(*u_full.step(it, "max", att, p, slot))

            def shift_transpose(it, att, p):
                pe.wait_ge(*shift_step.at(it, att, p, 1))
                ps = take(ring_u, it, ("shift", att, p), shift_out, (att, p))
                pe.transpose(ps[0:16, 0:P // 2].bitcast(BF16),
                             shift[p % 2][:, :, :].rearrange("p c g -> p (c g)"), ident_bf
                             ).then_inc(*u_full.step(it, "shift", att, p))

            def score_t(it, att, p, slot):
                if slot == 0:
                    pe.wait_ge(*shift_row[p % 2].at(it, att, p))
                ps = take(ring_g, it, ("scores", att, p, slot), exp_hi, (att, p, slot))
                for n, (hh, r) in enumerate(slot_tiles(p, slot)):
                    h = 2 * p + hh
                    kt, _, col, q0, q1 = tile_of(p, hh, r)
                    pe.matmul(ps[:, col:col + q1 - q0], k_stack[0:ROWS_P, h, P * kt:P * kt + P],
                              q_stack[0:ROWS_P, h, q0:q1], start=(n == 0), stop=False,
                              skip_group_check=True)
                    c, mask = (P * kt - q0, mask_low if forward(h) else mask_up)
                    ins = pe.matmul(ps[:, col + c:col + c + P], ident_bf, mask, start=False,
                                    stop=True, skip_group_check=True)
                ins.then_inc(*g_full.step(it, "scores", att, p, slot))

            def values(it, att, p, slot):
                pe.wait_ge(*exp_hi.at(it, att, p, slot))
                pe.wait_ge(*p_lo.at(it, att, p, slot))
                if slot == 0:
                    if p == 0:
                        pe.wait_ge(*v_step.at(it, att, 1, "third", prev=att == ATT))
                    take(ring_o, it, ("o", att, p), o_step, (att, p, "out"))
                ps = ring_o.bank("o", att, p)
                first = slot == 0
                for hh, r in slot_tiles(p, slot):
                    h = 2 * p + hh
                    kt, _, col, q0, q1 = tile_of(p, hh, r)
                    for qt in range(q0 // P, q1 // P):
                        g, c = 2 * qt + hh, col + P * qt - q0
                        for part in range(2):
                            ins = pe.matmul(ps[:, 64 * g:64 * g + 3 * HD + 1],
                                            ps_buf[item(p, slot) % NPS][part][:, c:c + P],
                                            v_parts[att - ATT][:, kt, h, 0:3 * HD + 1], start=first,
                                            stop=False, skip_group_check=True)
                            first = False
                ins.then_inc(*o_full.step(it, att, p, slot))

            def down(it, t):
                blk, j = tile(t)
                pe.wait_ge(*of(h_lo, it, t, 1))
                pe.wait_ge(*of(h_hi, it, t, 1))
                hs = hs_buf[j % 2]
                for i in range(NT):
                    if j == 0 and i % 2 == 0:
                        take(ring_y, it, ("y", blk, i // 2), x_new, ("ffn", blk, i // 2), late=blk == 3)
                    y = ring_y.bank("y", blk, i // 2)[:, D * (i % 2):D * (i % 2) + D]
                    ins = product(y, lambda c: hs[c][:, P * i:P * i + P],
                                  lambda c: w_down[:, c, j, :], j == 0 and i % 2 == 0, j == NM - 1)
                    if j == NM - 1 and i % 2 == 1:
                        ins.then_inc(*y_full.step(it, blk, i // 2))
                if j < NM - 1:
                    ins.then_inc(*h_used.step(it, t % (4 * NM)))

            def up_or_gate(it, t, ring, full, w, name, freed):
                blk, j = tile(t)
                xt = act_of(blk)
                ps = take(ring, it, (name, t), h_step, (t, freed))
                for d in range(ND):
                    ins = product(ps[:, :], lambda c: w[:, c, d, P * j:P * j + P],
                                  lambda c: xt[:, c, d, :], d == 0, d == ND - 1)
                ins.then_inc(*full.step(it, name, t))

            def weight(it, t):
                blk, j = tile(t)
                if j == NSH:
                    pe.wait_ge(*comb_out.at(it, blk))
                ps = take(ring_u, it, ("weight", t), h_step, (t, "h"))
                pe.matmul(ps[:, :], select[:, j - NSH, :], comb_t[blk % 2][:, :],
                          start=True, stop=True).then_inc(*u_full.step(it, "weight", t))

            def step(it, i):
                q, f = divmod(i, PERIOD)
                blk, j = tile(i)
                attend, ffn = attends(it, q), there(it, i)
                if first_time(it, i, 0):
                    pe.wait_ge(w_lo_done, 5)
                if first_time(it, i, 2):
                    pe.wait_ge(w_lo_done, 7)
                if first_time(it, i, NM):
                    pe.wait_ge(w_lo_done, 16)
                if first_time(it, i, PERIOD):
                    pe.wait_ge(aug_in, 32)
                    pe.wait_ge(ones_done, N_ONES)
                if attend and f in (0, HB):
                    for what in ("q", "k"):
                        pe.wait_ge(*scattered[ATT + q, what, f // HB].at(it, 5, prev=q == 0))
                rows = row_items(f) if attend else []
                if there(it, i - 2) and rows:
                    down(it, i - 2)
                if rows:
                    score(it, ATT + q, *rows[0])
                if attend and 2 <= f < H + 2 and f % 2 == 0:
                    shift_transpose(it, ATT + q, f // 2 - 1)
                if ffn:
                    if j == 0:
                        pe.wait_ge(*act_lo.at(it, ("xn", blk), ND - 1, prev=blk == 0))
                        pe.wait_ge(*act_hi.at(it, ("xn", blk), ND - 1, prev=blk == 0))
                    up_or_gate(it, i, ring_g, g_full, w_gate, "gate", "g")
                if there(it, i - 2) and not rows:
                    down(it, i - 2)
                items = score_items(f) if attend else []
                lagged = [before_item(*x, LAG) for x in items]
                if attend and f == 3 + 2 * NPAIR:
                    lagged = [divmod(5 * NPAIR - LAG + n, 5) for n in range(LAG)]

                def attend_to(n):
                    if n < len(items):
                        score_t(it, ATT + q, *items[n])
                    if n < len(lagged) and lagged[n]:
                        values(it, ATT + q, *lagged[n])

                attend_to(0)
                if ffn:
                    up_or_gate(it, i, ring_u, u_full, w_up, "up", "u" if j >= NSH else "h")
                for piece, to in preparation(it, i, MID):
                    prepare(it, piece, to)
                if rows:
                    score(it, ATT + q, *rows[1])
                attend_to(1)
                if len(rows) > 2:
                    score(it, ATT + q, *rows[2])
                if ffn and j >= NSH:
                    weight(it, i)
                attend_to(2)
                tail = attended(it, q)
                if tail and f == 0:
                    pe.wait_ge(*o_step.at(it, ATT + 1 - q, NPAIR - 1, "out", prev=q == 0))
                    transpose_act(it, ("o", ATT + 1 - q), o_tok)
                if tail and f == 1:
                    att = ATT + 1 - q
                    pe.wait_ge(*act_lo.at(it, ("o", att), ND - 1))
                    pe.wait_ge(*act_hi.at(it, ("o", att), ND - 1))
                    for half in range(2):
                        ps = take(ring_g, it, ("proj", att, half), x_new, ("att", att, half))
                        token_product(it, ps, half, act_t[1], 3
                                      ).then_inc(*g_full.step(it, "proj", att, half))
                for piece, to in preparation(it, i, END):
                    prepare(it, piece, to)

            def enter():
                for s in (act_hi, act_lo, x_new, h_step, h_hi, h_lo, qk_third, qk_step, exp_hi, max_done,
                          o_step, v_step, logits_out, route_step, comb_out, shift_out):
                    pe.wait_ge(*s.entered())

            pe.wait_ge(const_in, 16 * N_CONST)
            pe.wait_ge(w_lo_done, 1)
            program(pe, (u_full, g_full, y_full, o_full, h_used), step, enter)

        @block.scalar
        def _(act):
            xs = a["L0_attn_x"].rearrange("(i s) (t p) d -> i s p t d", s=2, p=P)
            os = out.rearrange("(i s) (t p) d -> i s p t d", s=2, p=P)

            def wait(event):
                if event:
                    act.wait_ge(*event)

            def load(it, q):
                wait(x_new.at(it, "ffn", 2 * q, 1))
                x_loaded[q].pass_over(act, it, q)
                act.dma_start(x_in[:, :, :], xs[(it + 1 + q) & (B // 2 - 1), 1 - q]
                              ).then_inc(*x_loaded[q].step(it, q))

            def store(it, q):
                act.wait_ge(*x_new.at(it, "ffn", (2 * q - 1) % 4, 1))
                act.dma_start(os[(it - 1 + q) & (B // 2 - 1), 1 - q], x_out[q][:, :, :]
                              ).then_inc(*stored[q].step(it, q))

            def hi_part(it, key, dst):
                for d in range(ND):
                    ring, full = transposed(key, d)
                    act.wait_ge(*full.at(it, key, d))
                    act.activation(dst[:, 0, d, :], ring.bank(key, d)[:, :], ACT.Copy
                                   ).then_inc(*act_hi.step(it, key, d))

            def qk_split(it, att, m):
                for n, what in enumerate(("q", "k")):
                    act.wait_ge(*g_full.at(it, what, att, m))
                    if m == 1:
                        wait(scattered[att, what, 0].at(it, 5))
                    else:
                        wait(scattered[2 * ATT + 1 - att, what, 1].at(it, 5, prev=att == ATT + 1))
                    act.activation(qk_part[n][:, 0, :], ring_g.bank(what, att, m)[:, :], ACT.Identity,
                                   bias=bias_qk[:, n, m:m + 1]).then_inc(*qk_first.step(it, att, what, m))
                for n, what in enumerate(("q", "k")):
                    act.wait_ge(*qk_step.at(it, att, what, m))
                    act.activation(qk_part[n][:, 1, :], rest[n], ACT.Copy
                                   ).then_inc(*qk_second.step(it, att, what, m))

            def prepare(it, piece, blk):
                if piece == "transpose":
                    if blk in (1, 3):
                        act.wait_ge(*g_full.at(it, "proj", ATT + 1 - blk // 2, 1))
                    elif kind(blk) == "att":
                        wait(u_full.at(it, "up", NM * 2 * (1 - (blk - ATT)) + NM - 1))
                    else:
                        wait(g_full.at(it, "k", ATT + blk // 2, 1))
                    hi_part(it, ("xn", blk), act_of(blk))
                elif piece == "a":
                    if kind(blk) == "att":
                        qk_split(it, blk, 0)
                    else:
                        act.wait_ge(*u_full.at(it, "logits", blk))
                        act.activation(logit_t, ring_u.bank("logits", blk)[:, :], ACT.Copy
                                       ).then_inc(*logits_out.step(it, blk))
                elif piece == "b":
                    if kind(blk) == "att":
                        v = [rest[half].rearrange("p (t h d) -> p t h d", t=2, d=HD) for half in range(2)]
                        dst = [v_parts[blk - ATT][:, 2 * half:2 * half + 2, :, :] for half in range(2)]
                        for half in range(2):
                            act.wait_ge(*v_step.at(it, blk, half, "bias"))
                            act.activation(dst[half][:, :, :, 0:HD], v[half], ACT.Copy
                                           ).then_inc(*v_first.step(it, blk, half))
                        for half in range(2):
                            act.wait_ge(*v_step.at(it, blk, half, "second"))
                            act.activation(dst[half][:, :, :, HD:2 * HD], v[half], ACT.Copy
                                           ).then_inc(*v_second.step(it, blk, half))
                    else:
                        act.wait_ge(*route_step.at(it, blk, "minus_max"))
                        act.activation(rt[:, 1], rt[:, 0], ACT.Exp).then_inc(*route_exp.step(it, blk))
                elif piece == "c":
                    if kind(blk) == "att":
                        qk_split(it, blk, 1)
                    else:
                        act.wait_ge(*u_full.at(it, "comb", blk))
                        act.activation(comb_t[blk % 2][:, :],
                                       ring_u.bank("comb", blk)[:, 0:S // 2].bitcast(F16), ACT.Copy
                                       ).then_inc(*comb_out.step(it, blk))

            def hi_of_h(it, t):
                j = t % NM
                act.wait_ge(*of(h_step, it, t, 0, "h"))
                if j < 2:
                    blk, prev = tile(t - 2)[0], t - 2 + 2 < 0
                    wait(y_full.at(it, blk, 1, prev=prev) if j == 1 else of(h_used, it, t - 2, 2))
                else:
                    wait(of(h_used, it, t - 2, 2))
                act.activation(hs_buf[j % 2][0], h_buf[j % 2], ACT.Copy
                               ).then_inc(*h_hi.step(it, t % (4 * NM)))

            def exponentials(it, att, p, slot):
                n = item(p, slot)
                act.wait_ge(*g_full.at(it, "scores", att, p, slot))
                old, prev = (divmod(n - 2, 5), False) if n >= 2 else ((NPAIR - 1, n + 3), att == ATT)
                wait(p_lo.at(it, att if n >= 2 else 2 * ATT + 1 - att, *old, prev=prev))
                src = ring_g.bank("scores", att, p, slot)[:, :]
                act.activation(p_buf[n % 2], src, ACT.Exp).then_inc(*exp_done.step(it, att, p, slot))
                if n >= NPS:
                    act.wait_ge(*o_full.at(it, att, *divmod(n - NPS, 5)))
                else:
                    wait(o_full.at(it, 2 * ATT + 1 - att, NPAIR - 1, 4, prev=att == ATT))
                act.activation(ps_buf[n % NPS][0], src, ACT.Exp).then_inc(*exp_hi.step(it, att, p, slot))

            def shift_to_stack(it, att, p):
                act.wait_ge(*u_full.at(it, "shift", att, p))
                if p >= 2:
                    act.wait_ge(*shift_row[p % 2].at(it, att, p - 2))
                act.activation(shift_t[p % 2][:, :], ring_u.bank("shift", att, p)[0:16, 0:P // 2]
                               .bitcast(BF16), ACT.Copy).then_inc(*shift_out.step(it, att, p))
                act.wait_ge(*shift_out.at(it, att, p))
                shift_row[p % 2].pass_over(act, it, att, p)
                act.dma_start(q_stack[ROWS_S:ROWS_P, 2 * p:2 * p + 2, :], shift_t[p % 2][:, :]
                              ).then_inc(*shift_row[p % 2].step(it, att, p))

            def step(it, i):
                q, f = divmod(i, PERIOD)
                attend = attends(it, q)
                if first_time(it, i, 0):
                    split_ffn()
                if first_time(it, i, NM):
                    split_attn()
                if attend and 2 <= f < H + 2 and f % 2 == 0:
                    shift_to_stack(it, ATT + q, f // 2 - 1)
                if there(it, i):
                    act.wait_ge(*g_full.at(it, "gate", i))
                    wait(of(h_step, it, i - 1, 0, "g"))
                    act.activation(th_buf[:, :], ring_g.bank("gate", i)[:, :], ACT.Tanh, scale=0.5
                                   ).then_inc(*tanh_done.step(it, i))
                if there(it, i - 1):
                    hi_of_h(it, i - 1)
                items = score_items(f) if attend else []
                if items:
                    exponentials(it, ATT + q, *items[0])
                for piece, blk in preparation(it, i, MID):
                    prepare(it, piece, blk)
                for p, slot in items[1:]:
                    exponentials(it, ATT + q, p, slot)
                if attended(it, q) and f == 0:
                    wait(u_full.at(it, "up", (2 * q * NM - 1) % (4 * NM), prev=q == 0))
                    hi_part(it, ("o", ATT + 1 - q), act_t[1])
                if f == 1 and there(it, i - 2):
                    store(it, q)
                if f == NM + 1 and there(it, i - 2):
                    load(it, q)
                for piece, blk in preparation(it, i, END):
                    prepare(it, piece, blk)

            def split_ffn():
                for i in range(6):
                    act.wait_ge(raw_in[i], 32 if i < 5 else 16)
                    act.activation(piece_of(i)[0], raw(i), ACT.Copy).then_inc(w_hi_done, 1)

            def split_attn():
                act.wait_ge(w_lo_done, 8)
                act.wait_ge(raw_in[6], 16 * 4)
                for w in range(4):
                    for d in range(ND):
                        act.activation(att_dst(0, w, d), att_src(w, d), ACT.Copy,
                                       scale=0.25 if w == 0 else 1.0).then_inc(w_hi_done, 1)

            act.dma_start(x_in[:, :, :], xs[0, 0]).then_inc(*x_loaded[1].step(-2, 1))
            act.wait_ge(const_in, 16 * N_CONST)
            act.wait_ge(filled, 1)
            act.activation(w_route[:, :, 0:E], raw_route, ACT.Copy).then_inc(w_hi_done, 1)
            program(act, (tanh_done, h_hi, act_hi, logits_out, route_exp, comb_out, qk_first, qk_second,
                          v_first, v_second, exp_done, exp_hi, shift_out, *shift_row, *x_loaded,
                          *stored), step)
            for q in range(2):
                act.wait_ge(*stored[q].at(ITERS + 1 - q, q))
                act.wait_ge(*x_loaded[q].at(ITERS, q, prev=True))

        @block.vector
        def _(dve):
            def wait(event):
                if event:
                    dve.wait_ge(*event)

            def lo_part(it, key, dst):
                for d in range(ND):
                    dve.wait_ge(*act_hi.at(it, key, d))
                    dve.tensor_tensor(dst[:, 1, d, :], transposed(key, d)[0].bank(key, d)[:, :],
                                      dst[:, 0, d, :].bitcast(F32), ALU.subtract
                                      ).then_inc(*act_lo.step(it, key, d))

            def norm_source(blk):
                if kind(blk) == "att":
                    return x_mid[blk - ATT]
                return x_out[1 - blk // 2] if blk in (1, 3) else x_in

            def moments(it, blk):
                x = norm_source(blk)
                if kind(blk) == "att":
                    dve.wait_ge(*x_new.at(it, "ffn", 2 * (ATT + 1 - blk), 1))
                elif blk in (1, 3):
                    dve.wait_ge(*x_new.at(it, "att", ATT + 1 - blk // 2, 1))
                else:
                    dve.wait_ge(*x_loaded[1 - blk // 2].at(it, 1 - blk // 2))
                for t in range(NT):
                    dve.bn_stats(stats[:, t, :], x[:, t, :]).then_inc(*norm_step.step(it, blk, "stats", t))
                dve.wait_ge(*norm_step.at(it, blk, "stats", NT - 1))
                even_mean, even_var, odd_mean, odd_var = (stats[:, :, c] for c in (1, 2, 4, 5))
                dve.tensor_tensor(mom[:, 0, :], even_mean, odd_mean, ALU.add
                                  ).then_inc(*norm_step.step(it, blk, "means"))
                dve.tensor_tensor(mom[:, 1, :], even_mean, odd_mean, ALU.subtract
                                  ).then_inc(*norm_step.step(it, blk, "apart"))
                dve.tensor_tensor(mom[:, 2, :], even_var, odd_var, ALU.add
                                  ).then_inc(*norm_step.step(it, blk, "within"))
                dve.wait_ge(*norm_step.at(it, blk, "apart"))
                dve.tensor_tensor(mom[:, 3, :], mom[:, 1, :], mom[:, 1, :], ALU.mult
                                  ).then_inc(*norm_step.step(it, blk, "square"))
                dve.wait_ge(*norm_step.at(it, blk, "within"))
                dve.tensor_scalar(mom[:, 4, :], mom[:, 2, :], 1.0 / D, EPS, ALU.mult, ALU.add
                                  ).then_inc(*norm_step.step(it, blk, "scaled"))
                dve.tensor_scalar(mean[:, :], mom[:, 0, :], 0.5, None, ALU.mult
                                  ).then_inc(*norm_step.step(it, blk, "mean"))
                dve.wait_ge(*norm_step.at(it, blk, "scaled"))
                dve.scalar_tensor_tensor(var_eps[:, :], mom[:, 3, :], 0.25, mom[:, 4, :], ALU.mult,
                                         ALU.add).then_inc(*norm_step.step(it, blk, "eps"))

            def layer_norm(it, blk):
                x = norm_source(blk)
                dve.wait_ge(*rstd_done.at(it, blk))
                if kind(blk) == "att":
                    wait(u_full.at(it, "route", 2 * (ATT + 1 - blk) + 1))
                elif blk in (1, 3):
                    wait(u_full.at(it, "route", blk - 1, prev=blk == 1))
                else:
                    wait(qk_third.at(it, ATT + blk // 2, "q", 1))
                    wait(qk_third.at(it, ATT + blk // 2, "k", 1))
                    wait(qk_second.at(it, ATT + blk // 2, "k", 1))
                for t in range(NT):
                    dve.tensor_scalar(xn_tok[:, t, :], x[:, t, :], mean[:, t:t + 1], rstd[:, t:t + 1],
                                      ALU.subtract, ALU.mult).then_inc(*norm_step.step(it, blk, "apply", t))

            def qk_rests(it, att, m):
                for n, what in enumerate(("q", "k")):
                    dve.wait_ge(*qk_first.at(it, att, what, m))
                    if m == 1:
                        dve.wait_ge(*v_step.at(it, att, n, "third"))
                    dve.scalar_tensor_tensor(rest[n], ring_g.bank(what, att, m)[:, :],
                                             bias_qk[:, n, m:m + 1], qk_part[n][:, 0, :],
                                             ALU.add, ALU.subtract).then_inc(*qk_step.step(it, att, what, m))

            def v_rests(it, att):
                v = [rest[half].rearrange("p (t h d) -> p t h d", t=2, d=HD) for half in range(2)]
                dst = [v_parts[att - ATT][:, 2 * half:2 * half + 2, :, :] for half in range(2)]
                for half in range(2):
                    dve.wait_ge(*g_full.at(it, "v", att, half))
                    dve.wait_ge(*qk_third.at(it, att, ("q", "k")[half], 0))
                    dve.tensor_tensor(rest[half].rearrange("p (t d) -> p t d", d=D),
                                      ring_g.bank("v", att, half)[:, :].rearrange(
                        "p (t d) -> p t d", d=D), bias_v[:, :].unsqueeze(1).broadcast_to((P, 2, D)),
                        ALU.add).then_inc(*v_step.step(it, att, half, "bias"))
                for half in range(2):
                    dve.wait_ge(*v_first.at(it, att, half))
                    dve.tensor_tensor(v[half], v[half], dst[half][:, :, :, 0:HD], ALU.subtract
                                      ).then_inc(*v_step.step(it, att, half, "second"))
                for half in range(2):
                    dve.wait_ge(*v_second.at(it, att, half))
                    dve.tensor_tensor(dst[half][:, :, :, 2 * HD:3 * HD], v[half],
                                      dst[half][:, :, :, HD:2 * HD], ALU.subtract
                                      ).then_inc(*v_step.step(it, att, half, "third"))

            def best(it, blk):
                def done(name, ins):
                    ins.then_inc(*route_step.step(it, blk, name))
                    dve.wait_ge(*route_step.at(it, blk, name))

                d, _, pick, sel, _, _ = (rt[:, i] for i in range(6))

                def wide(i):
                    return top[:, i, :].unsqueeze(2).broadcast_to((P, NT, E))

                dve.wait_ge(*u_full.at(it, "route", blk))
                done("sum", dve.tensor_reduce(logit[:, :, :], ring_u.bank("route", blk)[:, :]
                     .rearrange("p (t m) -> p t m", m=P)[:, :, 0:2 * E]
                     .rearrange("p t (c e) -> p t e c", e=E), X, ALU.add))
                done("max", dve.tensor_reduce(top[:, 0, :], logit[:, :, :], X, ALU.max))
                done("minus_max", dve.tensor_tensor(d, logit[:, :, :], wide(0), ALU.subtract))
                done("hit1", dve.scalar_tensor_tensor(pick, d, 0.0, rev, ALU.is_ge, ALU.mult))
                done("low1", dve.tensor_reduce(top[:, 1, :], pick, X, ALU.max))
                done("one1", dve.tensor_tensor(sel, pick, wide(1), ALU.is_equal))

            def second(it, blk):
                def done(name, ins):
                    ins.then_inc(*route_step.step(it, blk, name))
                    dve.wait_ge(*route_step.at(it, blk, name))

                d, e, pick, sel, tmp, one = (rt[:, i] for i in range(6))

                def wide(i):
                    return top[:, i, :].unsqueeze(2).broadcast_to((P, NT, E))

                done("rest", dve.scalar_tensor_tensor(tmp, sel, -BIG, d, ALU.mult, ALU.add))
                done("max2", dve.tensor_reduce(top[:, 2, :], tmp, X, ALU.max))
                done("hit2", dve.tensor_tensor(pick, tmp, wide(2), ALU.is_equal))
                done("rev2", dve.tensor_tensor(pick, pick, rev, ALU.mult))
                done("low2", dve.tensor_reduce(top[:, 3, :], pick, X, ALU.max))
                done("one2", dve.tensor_tensor(one, pick, wide(3), ALU.is_equal))
                done("both", dve.tensor_tensor(sel, sel, one, ALU.add))

            def combine(it, blk):
                def done(name, ins):
                    ins.then_inc(*route_step.step(it, blk, name))
                    dve.wait_ge(*route_step.at(it, blk, name))

                _, e, _, sel, tmp, one = (rt[:, i] for i in range(6))

                def wide(i):
                    return top[:, i, :].unsqueeze(2).broadcast_to((P, NT, E))

                dve.wait_ge(*route_exp.at(it, blk, prev=blk == 0))
                done("chosen", dve.tensor_tensor(tmp, sel, e, ALU.mult))
                done("sum2", dve.tensor_reduce(top[:, 4, :], tmp, X, ALU.add))
                done("sum16", dve.tensor_reduce(top[:, 5, :], e, X, ALU.add))
                done("den", dve.scalar_tensor_tensor(top[:, 6, :], top[:, 5, :], 1e-9, top[:, 4, :],
                                                     ALU.mult, ALU.add))
                done("rden", dve.reciprocal(top[:, 7, :], top[:, 6, :]))
                done("comb", dve.tensor_tensor(one, tmp, wide(7), ALU.mult))
                done("hi", dve.tensor_copy(comb[:, :, 0:E], one))
                done("lo", dve.tensor_tensor(comb[:, :, E:2 * E], one, comb[:, :, 0:E], ALU.subtract))

            def prepare(it, piece, blk):
                if piece == "moments":
                    moments(it, blk)
                elif piece == "norm":
                    layer_norm(it, blk)
                elif piece == "transpose":
                    lo_part(it, ("xn", blk), act_of(blk))
                elif kind(blk) == "att":
                    if piece == "b":
                        v_rests(it, blk)
                    else:
                        qk_rests(it, blk, 0 if piece == "a" else 1)
                elif piece == "b":
                    best(it, blk)
                elif piece == "b2":
                    second(it, blk)
                elif piece == "b3":
                    combine(it, blk)

            def first_update(it, q):
                for half in range(2):
                    dve.wait_ge(*y_full.at(it, 2 * q, half))
                    wait(x_new.at(it, "att", ATT + 1 - q, half))
                    at = slice(2 * half, 2 * half + 2)
                    y = ring_y.bank("y", 2 * q, half)[:, :].rearrange("p (t d) -> p t d", d=D)
                    dve.scalar_tensor_tensor(x_mid[1 - q][:, at, :], y, 0.25, x_in[:, at, :], ALU.mult,
                                             ALU.add).then_inc(*x_new.step(it, "ffn", 2 * q, half))

            def second_update(it, q):
                blk = (2 * q - 1) % 4
                for half in range(2):
                    dve.wait_ge(*y_full.at(it, blk, half))
                    x = x_out[q % 2][:, 2 * half:2 * half + 2, :]
                    y = ring_y.bank("y", blk, half)[:, :].rearrange("p (t d) -> p t d", d=D)
                    dve.scalar_tensor_tensor(x, y, 0.25, x, ALU.mult, ALU.add
                                             ).then_inc(*x_new.step(it, "ffn", blk, half))

            def attention_update(it, q):
                s = 1 - q
                for half in range(2):
                    dve.wait_ge(*g_full.at(it, "proj", ATT + s, half))
                    if half == 0:
                        dve.wait_ge(*bias_added.at(it, ATT + s, prev=True))
                        wait(stored[s].at(it, s, prev=q == 0))
                    at = slice(2 * half, 2 * half + 2)
                    y = ring_g.bank("proj", ATT + s, half)[:, :].rearrange("p (t d) -> p t d", d=D)
                    dve.tensor_tensor(x_out[s][:, at, :], y, x_mid[s][:, at, :], ALU.add
                                      ).then_inc(*x_new.step(it, "att", ATT + s, half))

            def maximum(it, att, p, slot):
                dve.wait_ge(*u_full.at(it, "max", att, p, slot))
                if slot == 0:
                    wait(shift_step.at(it, *((att, p - 2) if p >= 2 else
                                             (2 * ATT + 1 - att, NPAIR - 2 + p)), 1,
                                       prev=p < 2 and att == ATT))
                src = ring_u.bank("max", att, p, slot)
                tiles = slot_tiles(p, slot)
                if slot == 2:
                    ins = dve.tensor_reduce(
                        row_max[p % 2][:, :].rearrange("p (h t) -> p t h", t=NT)[:, row_tile(p, *tiles[0])],
                        src[:, :].rearrange("p (h s) -> p h s", h=2), X, ALU.max)
                else:
                    for hh, r in tiles:
                        _, _, col, q0, q1 = tile_of(p, hh, r)
                        n = NT * hh + row_tile(p, hh, r)
                        ins = dve.tensor_reduce(row_max[p % 2][:, n:n + 1], src[:, col:col + q1 - q0],
                                                X, ALU.max)
                ins.then_inc(*max_done.step(it, att, p, slot))

            def shifts(it, att, p):
                dve.wait_ge(*max_done.at(it, att, p, 4))
                wait(u_full.at(it, "shift", *((att, p - 2) if p >= 2 else
                                              (2 * ATT + 1 - att, NPAIR - 2 + p)),
                               prev=p < 2 and att == ATT))
                dve.tensor_scalar(shift[p % 2][:, 0, :], row_max[p % 2][:, :], -1.0, None, ALU.mult
                                  ).then_inc(*shift_step.step(it, att, p, 0))
                dve.wait_ge(*shift_step.at(it, att, p, 0))
                dve.scalar_tensor_tensor(shift[p % 2][:, 1, :], row_max[p % 2][:, :], -1.0,
                                         shift[p % 2][:, 0, :], ALU.mult, ALU.subtract
                                         ).then_inc(*shift_step.step(it, att, p, 1))

            def normalise(it, att, p):
                dve.wait_ge(*o_full.at(it, att, p, 4))
                if p >= 1:
                    dve.wait_ge(*o_step.at(it, att, p - 1, "out"))
                else:
                    wait(g_full.at(it, ("o", 2 * ATT + 1 - att), ND - 1))
                ps = ring_o.bank("o", att, p)[:, :].rearrange("p (g c) -> p g c", c=64)
                dve.tensor_reduce(o_sum[:, :, :], ps[:, :, 0:3 * HD].rearrange(
                    "p g (c d) -> p g d c", c=PARTS), X, ALU.add).then_inc(*o_step.step(it, att, p, "sum"))
                dve.reciprocal(o_rden[:, :], ps[:, :, 3 * HD]).then_inc(*o_step.step(it, att, p, "rden"))
                dve.wait_ge(*o_step.at(it, att, p, "rden"))
                dve.tensor_tensor(
                    o_tok[:, :, 2 * HD * p:2 * HD * p + 2 * HD].rearrange("p t (h d) -> p t h d", h=2),
                    o_sum[:, :, :].rearrange("p (t h) d -> p t h d", h=2),
                    o_rden[:, :].rearrange("p (t h) -> p t h", h=2).unsqueeze(3)
                    .broadcast_to((P, NT, 2, HD)), ALU.mult).then_inc(*o_step.step(it, att, p, "out"))

            def hidden(it, t, part):
                j = t % NM
                h = h_buf[j % 2]
                if part == 0:
                    dve.wait_ge(*tanh_done.at(it, t))
                    wait(of(h_hi, it, t - 2, 1))
                    wait(of(h_lo, it, t - 2, 1))
                    dve.scalar_tensor_tensor(h, th_buf[:, :], 1.0, ring_g.bank("gate", t)[:, :],
                                             ALU.add, ALU.mult).then_inc(*h_step.step(it, t, "g"))
                elif part == 1:
                    dve.wait_ge(*h_step.at(it, t, "g"))
                    dve.wait_ge(*u_full.at(it, "up", t))
                    dve.tensor_tensor(h, ring_u.bank("up", t)[:, :], h, ALU.mult
                                      ).then_inc(*h_step.step(it, t, "u" if j >= NSH else "h"))
                elif j >= NSH:
                    dve.wait_ge(*h_step.at(it, t, "u"))
                    dve.wait_ge(*u_full.at(it, "weight", t))
                    dve.tensor_tensor(h, ring_u.bank("weight", t)[:, :], h, ALU.mult
                                      ).then_inc(*h_step.step(it, t, "h"))

            def step(it, i):
                q, f = divmod(i, PERIOD)
                attend, ffn = attends(it, q), there(it, i)
                if first_time(it, i, 0):
                    split_ffn()
                if first_time(it, i, NM):
                    split_attn()
                rows = row_items(f) if attend else []
                if rows:
                    maximum(it, ATT + q, *rows[0])
                if f == 1 and there(it, i - 2):
                    second_update(it, q)
                if f == NM + 1 and there(it, i - 2):
                    first_update(it, q)
                if ffn:
                    hidden(it, i, 0)
                if ffn:
                    hidden(it, i, 1)
                for piece, blk in preparation(it, i, MID):
                    prepare(it, piece, blk)
                if rows:
                    maximum(it, ATT + q, *rows[1])
                if len(rows) > 2:
                    maximum(it, ATT + q, *rows[2])
                if rows and f % 2 == 1:
                    shifts(it, ATT + q, f // 2)
                if ffn:
                    hidden(it, i, 2)
                if attend and 5 <= f <= 3 + 2 * NPAIR and f % 2 == 1:
                    normalise(it, ATT + q, (f - 5) // 2)
                if attended(it, q) and f == 0:
                    lo_part(it, ("o", ATT + 1 - q), act_t[1])
                if attended(it, q) and f == 1:
                    attention_update(it, q)
                for piece, blk in preparation(it, i, END):
                    prepare(it, piece, blk)

            def split_ffn():
                for i in range(6):
                    dve.wait_ge(w_hi_done, i + 2)
                    dve.tensor_tensor(piece_of(i)[1], raw(i), piece_of(i)[0].bitcast(F32), ALU.subtract
                                      ).then_inc(w_lo_done, 1)

            def split_attn():
                dve.wait_ge(ones_done, N_ONES)
                dve.wait_ge(bias_in, 16 * N_BIAS)
                dve.tensor_scalar(bias_qk[:, 0, :], bias_qk[:, 0, :], 0.25, None, ALU.mult
                                  ).then_inc(w_lo_done, 1)
                for n in range(4 * ND):
                    w, d = divmod(n, ND)
                    dve.wait_ge(w_hi_done, n + 8)
                    if w == 0:
                        for m in range(ND):
                            ins = dve.scalar_tensor_tensor(
                                att_dst(1, w, d)[:, m], att_src(w, d)[:, m], 0.25,
                                att_dst(0, w, d)[:, m].bitcast(F32), ALU.mult, ALU.subtract)
                    else:
                        ins = dve.tensor_tensor(att_dst(1, w, d), att_src(w, d),
                                                att_dst(0, w, d).bitcast(F32), ALU.subtract)
                    ins.then_inc(w_lo_done, 1)

            dve.memset(w_route[:, :, :].bitcast(F32), 0.0).then_inc(filled, 1)
            dve.memset(comb[:, :, :], 0.0).then_inc(filled, 1)
            dve.wait_ge(filled, 2)
            dve.wait_ge(const_in, 16 * N_CONST)
            dve.wait_ge(w_hi_done, 1)
            dve.tensor_tensor(w_route[:, :, E:2 * E], raw_route, w_route[:, :, 0:E].bitcast(F32),
                              ALU.subtract).then_inc(w_lo_done, 1)
            program(dve, (h_step, act_lo, norm_step, route_step, qk_step, v_step, max_done, shift_step,
                          o_step, x_new), step)

        @block.gpsimd
        def _(pool):
            def prepare(it, piece, blk):
                if piece == "moments":
                    pool.wait_ge(*norm_step.at(it, blk, "eps"))
                    pool.tensor_tensor(rstd[:, :], var_eps[:, :], minus_half[:, :], ALU.pow
                                       ).then_inc(*rstd_done.step(it, blk))
                elif kind(blk) == "att" and piece in ("a", "c"):
                    m = 0 if piece == "a" else 1
                    for n, what in enumerate(("q", "k")):
                        pool.wait_ge(*qk_second.at(it, blk, what, m))
                        pool.tensor_tensor(qk_part[n][:, 2, :], rest[n], qk_part[n][:, 1, :],
                                           ALU.subtract).then_inc(*qk_third.step(it, blk, what, m))
                elif kind(blk) == "att" and piece == "transpose":
                    pool.wait_ge(*norm_step.at(it, blk, "apply", NT - 1))
                    x = x_mid[blk - ATT]
                    pool.tensor_tensor(x[:, :, :], x[:, :, :],
                                       bias_f[:, :].unsqueeze(1).broadcast_to((P, NT, D)), ALU.add
                                       ).then_inc(*bias_added.step(it, blk))

            def low_probabilities(it, att, p, slot):
                n = item(p, slot)
                pool.wait_ge(*exp_hi.at(it, att, p, slot))
                pool.tensor_tensor(ps_buf[n % NPS][1], p_buf[n % 2], ps_buf[n % NPS][0],
                                   ALU.subtract).then_inc(*p_lo.step(it, att, p, slot))

            def step(it, i):
                q, f = divmod(i, PERIOD)
                if there(it, i - 1):
                    t = (i - 1) % (4 * NM)
                    j = t % NM
                    pool.wait_ge(*h_hi.at(it, t))
                    pool.tensor_tensor(hs_buf[j % 2][1], h_buf[j % 2], hs_buf[j % 2][0].bitcast(F32),
                                       ALU.subtract).then_inc(*h_lo.step(it, t))
                items = score_items(f) if attends(it, q) else []
                if items:
                    low_probabilities(it, ATT + q, *items[0])
                for piece, blk in preparation(it, i, MID):
                    prepare(it, piece, blk)
                for p, slot in items[1:]:
                    low_probabilities(it, ATT + q, p, slot)
                for piece, blk in preparation(it, i, END):
                    prepare(it, piece, blk)

            pool.memset(minus_half[:, :], -0.5).then_inc(ones_done, 1)
            for v in v_parts:
                pool.memset(v[:, :, :, :], 1.0).then_inc(ones_done, 1)
            pool.memset(x_out[0][:, :, :], 0.0).then_inc(ones_done, 1)
            pool.wait_ge(ones_done, N_ONES)
            program(pool, (rstd_done, h_lo, qk_third, p_lo, bias_added), step)


_INS = ["L0_attn_x", "L0_attn_Wq", "L0_attn_bq", "L0_attn_Wk", "L0_attn_bk", "L0_attn_Wv", "L0_attn_bv",
        "L0_attn_Wf", "L0_attn_bf", "L0_ffn_router_w", "L0_ffn_wg_r", "L0_ffn_wu_r", "L0_ffn_wd_r",
        "L0_ffn_wg_s", "L0_ffn_wu_s", "L0_ffn_wd_s"]


def constants():
    import numpy as np

    bf16 = mybir.dt.np(BF16)
    eye = np.eye(P, dtype=np.float32)
    rev = np.tile(np.arange(E, 0, -1, dtype=np.float32), NT)
    c32 = np.concatenate([eye, np.broadcast_to(rev, (P, NT * E))], 1)
    select = np.zeros((P, 8, P), np.float32)
    for j in range(8):
        for m in range(P):
            for c in range(2):
                select[c * E + 2 * j + m // ME, j, m] = 1.0
    c16 = np.concatenate([eye, select.reshape(P, -1)], 1).astype(np.float16)
    neg = np.float32(-1e9)
    cbf = np.concatenate([eye, np.triu(np.full((P, P), neg), 1), np.tril(np.full((P, P), neg), -1)],
                         1).astype(bf16)
    half = H // 2
    base = np.float32(24.0 ** (1.0 / half))
    slopes = (np.float32(1.0) / base ** np.arange(1, half + 1, dtype=np.float32)).astype(np.float32)
    slopes = np.concatenate([slopes, -slopes])
    parts, rest = [], slopes
    for _ in range(PARTS):
        parts.append(rest.astype(bf16))
        rest = rest - parts[-1].astype(np.float32)
    q_rows = np.broadcast_to(np.stack(parts)[:, :, None], (PARTS, H, S))
    pos = np.broadcast_to((np.arange(S) - S // 2).astype(np.float32), (PARTS, H, S))
    k_rows = np.concatenate([pos, np.ones((2, H, S), np.float32)]).astype(bf16)
    return {"c32": c32.astype(np.float32), "c16": c16, "cbf": cbf,
            "q_rows": np.ascontiguousarray(q_rows), "k_rows": k_rows}


def kernel(**inputs):
    import numpy as _np
    import concourse.bacc as _bacc
    from concourse import mybir as _mybir
    from concourse.bass_utils import run_bass_kernel_spmd as _run

    arrays = {n: _np.ascontiguousarray(inputs[n]) for n in _INS}
    arrays.update(constants())
    book = Book()
    for final in (False, True):
        book.final = final
        nc = _bacc.Bacc("TRN2", target_bir_lowering=False, num_devices=1)
        aps = {n: nc.dram_tensor(f"in_{n}", v.shape, _mybir.dt.from_np(v.dtype), kind="ExternalInput").ap()
               for n, v in arrays.items()}
        out = nc.dram_tensor("out_0_dram", (B, S, D), F32, kind="ExternalOutput").ap()
        build(nc, book, aps, out)
    r = _run(nc, [{f"in_{n}": v for n, v in arrays.items()}], core_ids=[0])
    return r.results[0]["out_0_dram"]
```
